# Optimizing a Trainium2 kernel written in Bass

```python
import numpy as np
import jax
import jax.numpy as jnp

def _softmax(x, axis=-1):
    return jax.nn.softmax(x, axis=axis)

def _gelu(x):
    return jax.nn.gelu(x, approximate=True)

def _silu(x):
    return jax.nn.silu(x)

def _sigmoid(x):
    return jax.nn.sigmoid(x)

def _layernorm(x, axis=-1, eps=1e-05):
    m = jnp.mean(x, axis=axis, keepdims=True)
    v = jnp.var(x, axis=axis, keepdims=True)
    return (x - m) / jnp.sqrt(v + eps)

def _scatter_add(tgt, idx, src, axis=0):
    return tgt.at[idx].add(src)

def _segment_sum(src, seg, n):
    return jax.ops.segment_sum(src, seg, n)
kernel_name = 'mk_cond_resid_d4_seqx_r4_b1aca9'

def setup_inputs(seed: int=0):
    np.random.seed(seed)
    _w = jnp.asarray

    def _rec_inputs():
        import jax
        import jax.numpy as jnp
        _rk = jax.random.key(seed)
        x = 7.22e-05 + 1 * jax.random.normal(jax.random.fold_in(_rk, 1), (64, 64, 256), jnp.float32)
        _lenS = 64 - jax.random.randint(jax.random.fold_in(_rk, 7), (64,), 0, max(1, 64 // 4) + 1, jnp.int32)
        _lenS2 = 64 - jax.random.randint(jax.random.fold_in(_rk, 8), (64,), 0, max(1, 64 // 4) + 1, jnp.int32)
        cond_8 = -0.104238 + 1.01173 * jax.random.normal(jax.random.fold_in(_rk, 11), (64, 8), jnp.float32)
        return (x, cond_8)
    x, cond_8 = _rec_inputs()

    def _L0_cond_setup():
        import jax, jax.numpy as jnp
        import numpy as np
        TOP_K = 2
        NUM_MOE_LAYERS = 12

        def _gemma_mlp(x, gate_w, up_w, down_w):
            g = jnp.einsum('bsh,hi->bsi', x, gate_w)
            u = jnp.einsum('bsh,hi->bsi', x, up_w)
            return jnp.einsum('bsi,ih->bsh', jax.nn.gelu(g, approximate=True) * u, down_w)
        key = jax.random.key(seed)
        ks = jax.random.split(key, 8)
        B, S, H, I, E = (32, 64, 256, 1024, 8)
        std = 0.02
        return {'x': jax.random.normal(ks[0], (B, S, H), jnp.float32), 'router_logits': jax.random.normal(ks[1], (B, E), jnp.float32), 'skill_gate': jax.random.normal(ks[2], (E, H, I), jnp.float32) * std, 'skill_up': jax.random.normal(ks[3], (E, H, I), jnp.float32) * std, 'skill_down': jax.random.normal(ks[4], (E, I, H), jnp.float32) * std, 'shared_gate': jax.random.normal(ks[5], (H, I), jnp.float32) * std, 'shared_up': jax.random.normal(ks[6], (H, I), jnp.float32) * std, 'shared_down': jax.random.normal(ks[7], (I, H), jnp.float32) * std}
    _L0_cond_all = _L0_cond_setup()
    _L0_cond_in = {k: v for k, v in _L0_cond_all.items() if k in ('skill_gate', 'skill_up', 'skill_down', 'shared_gate', 'shared_up', 'shared_down')}
    del _L0_cond_all

    def _L1_cond_setup():
        import jax, jax.numpy as jnp
        import numpy as np
        key = jax.random.key(seed)
        k1, k2, k3, k4, k5 = jax.random.split(key, 5)
        B, N, T, O, G = (32, 64, 256, 256, 8)
        x = jax.random.normal(k1, (B, N, T), dtype=jnp.float32)
        y = jax.random.uniform(k2, (B, G), dtype=jnp.float32)
        weight = jax.random.normal(k3, (G, O, T), dtype=jnp.float32) * (1.0 / np.sqrt(T))
        mask = jax.random.uniform(k4, (O, T), dtype=jnp.float32)
        bias = jax.random.normal(k5, (O,), dtype=jnp.float32)
        return {'x': x, 'y': y, 'weight': weight, 'mask': mask, 'bias': bias}
    _L1_cond_all = _L1_cond_setup()
    _L1_cond_in = {k: v for k, v in _L1_cond_all.items() if k in ('weight', 'mask', 'bias')}
    del _L1_cond_all

    def _L2_cond_setup():
        import jax, jax.numpy as jnp
        import numpy as np
        R = 16
        ALPHA = 32.0
        SCALING = ALPHA / R
        key = jax.random.key(seed)
        ks = jax.random.split(key, 6)
        B, T, C, O, E = (16, 375, 256, 256, 8)
        x = jax.random.normal(ks[0], (B, T, C), dtype=jnp.float32)
        w = jax.random.uniform(ks[1], (B, E), dtype=jnp.float32)
        W_base = jax.random.normal(ks[2], (O, C), dtype=jnp.float32) * 0.02
        b_base = jax.random.normal(ks[3], (O,), dtype=jnp.float32) * 0.02
        As = jax.random.normal(ks[4], (E, R, C), dtype=jnp.float32) * 0.02
        Bs = jax.random.normal(ks[5], (E, O, R), dtype=jnp.float32) * 0.02
        return {'x': x, 'w': w, 'W_base': W_base, 'b_base': b_base, 'As': As, 'Bs': Bs}
    _L2_cond_all = _L2_cond_setup()
    _L2_cond_in = {k: v for k, v in _L2_cond_all.items() if k in ('W_base', 'b_base', 'As', 'Bs')}
    del _L2_cond_all

    def _L3_cond_setup():
        import jax, jax.numpy as jnp
        import numpy as np
        B, S, D = (16, 512, 256)
        E, H = (8, 512)
        key = jax.random.key(seed)
        ks = jax.random.split(key, 8)
        scale = 0.02
        x = jax.random.normal(ks[0], (B, S, D), dtype=jnp.float32)
        opcode_onehot = jax.random.uniform(ks[1], (B, E), dtype=jnp.float32)
        W_up = jax.random.normal(ks[2], (E, H, D), dtype=jnp.float32) * scale
        b_up = jnp.zeros((E, H), dtype=jnp.float32)
        W_gate = jax.random.normal(ks[3], (E, H, D), dtype=jnp.float32) * scale
        b_gate = jnp.zeros((E, H), dtype=jnp.float32)
        W_down = jax.random.normal(ks[4], (E, D, H), dtype=jnp.float32) * scale
        b_down = jnp.zeros((E, D), dtype=jnp.float32)
        return {'x': x, 'opcode_onehot': opcode_onehot, 'W_up': W_up, 'b_up': b_up, 'W_gate': W_gate, 'b_gate': b_gate, 'W_down': W_down, 'b_down': b_down}
    _L3_cond_all = _L3_cond_setup()
    _L3_cond_in = {k: v for k, v in _L3_cond_all.items() if k in ('W_up', 'b_up', 'W_gate', 'b_gate', 'W_down', 'b_down')}
    del _L3_cond_all
    return {'x': x, 'cond_8': cond_8, 'L0_cond_skill_gate': _L0_cond_in['skill_gate'], 'L0_cond_skill_up': _L0_cond_in['skill_up'], 'L0_cond_skill_down': _L0_cond_in['skill_down'], 'L0_cond_shared_gate': _L0_cond_in['shared_gate'], 'L0_cond_shared_up': _L0_cond_in['shared_up'], 'L0_cond_shared_down': _L0_cond_in['shared_down'], 'L1_cond_weight': _L1_cond_in['weight'], 'L1_cond_mask': _L1_cond_in['mask'], 'L1_cond_bias': _L1_cond_in['bias'], 'L2_cond_W_base': _L2_cond_in['W_base'], 'L2_cond_b_base': _L2_cond_in['b_base'], 'L2_cond_As': _L2_cond_in['As'], 'L2_cond_Bs': _L2_cond_in['Bs'], 'L3_cond_W_up': _L3_cond_in['W_up'], 'L3_cond_b_up': _L3_cond_in['b_up'], 'L3_cond_W_gate': _L3_cond_in['W_gate'], 'L3_cond_b_gate': _L3_cond_in['b_gate'], 'L3_cond_W_down': _L3_cond_in['W_down'], 'L3_cond_b_down': _L3_cond_in['b_down']}

def reference(x, cond_8, L0_cond_skill_gate, L0_cond_skill_up, L0_cond_skill_down, L0_cond_shared_gate, L0_cond_shared_up, L0_cond_shared_down, L1_cond_weight, L1_cond_mask, L1_cond_bias, L2_cond_W_base, L2_cond_b_base, L2_cond_As, L2_cond_Bs, L3_cond_W_up, L3_cond_b_up, L3_cond_W_gate, L3_cond_b_gate, L3_cond_W_down, L3_cond_b_down):
    import jax
    import jax.numpy as jnp

    def _L0_cond_ref(x, router_logits, skill_gate, skill_up, skill_down, shared_gate, shared_up, shared_down):
        import jax, jax.numpy as jnp
        import numpy as np
        TOP_K = 2
        NUM_MOE_LAYERS = 12

        def _gemma_mlp(x, gate_w, up_w, down_w):
            g = jnp.einsum('bsh,hi->bsi', x, gate_w)
            u = jnp.einsum('bsh,hi->bsi', x, up_w)
            return jnp.einsum('bsi,ih->bsh', jax.nn.gelu(g, approximate=True) * u, down_w)
        B = x.shape[0]
        E = skill_gate.shape[0]
        rw = jax.nn.softmax(router_logits.astype(jnp.float32), axis=-1)
        w, sel = jax.lax.top_k(rw, TOP_K)
        w = w / w.sum(axis=-1, keepdims=True)
        w = w.astype(x.dtype)
        scale = 1.0 / NUM_MOE_LAYERS
        w = scale * w + (1.0 - scale) * jax.lax.stop_gradient(w)
        dense_w = jnp.zeros((B, E), x.dtype).at[jnp.arange(B)[:, None], sel].add(w)

        def step(acc, params):
            g, u, d, we = params
            return (acc + we[:, None, None] * _gemma_mlp(x, g, u, d), None)
        out, _ = jax.lax.scan(step, jnp.zeros_like(x), (skill_gate, skill_up, skill_down, dense_w.T))
        out = out + _gemma_mlp(x, shared_gate, shared_up, shared_down)
        return out

    def _L1_cond_ref(x, y, weight, mask, bias):
        import jax, jax.numpy as jnp
        import numpy as np
        masked_w = weight * mask[None, :, :]
        w_bot = jnp.einsum('bg,got->bot', y, masked_w)
        return jnp.einsum('bnt,bot->bno', x, w_bot) + bias

    def _L2_cond_ref(x, w, W_base, b_base, As, Bs):
        import jax, jax.numpy as jnp
        import numpy as np
        R = 16
        ALPHA = 32.0
        SCALING = ALPHA / R
        out = jnp.einsum('btc,oc->bto', x, W_base) + b_base
        h = jnp.einsum('btc,erc->bter', x, As)
        lora = jnp.einsum('bter,eor,be->bto', h, Bs, w)
        return out + lora * SCALING

    def _L3_cond_ref(x, opcode_onehot, W_up, b_up, W_gate, b_gate, W_down, b_down):
        import jax, jax.numpy as jnp
        import numpy as np
        B, S, D = (16, 512, 256)
        E, H = (8, 512)
        expert = jnp.argmax(opcode_onehot, axis=-1)
        wu, bu = (W_up[expert], b_up[expert])
        wg, bg = (W_gate[expert], b_gate[expert])
        wd, bd = (W_down[expert], b_down[expert])
        up = jnp.einsum('bsd,bhd->bsh', x, wu) + bu[:, None, :]
        gate = jnp.einsum('bsd,bhd->bsh', x, wg) + bg[:, None, :]
        hidden = jax.nn.silu(up) * gate
        out = jnp.einsum('bsh,bdh->bsd', hidden, wd) + bd[:, None, :]
        return out
    x = x + _L0_cond_ref(x, cond_8, L0_cond_skill_gate, L0_cond_skill_up, L0_cond_skill_down, L0_cond_shared_gate, L0_cond_shared_up, L0_cond_shared_down)
    x = x + _L1_cond_ref(x, cond_8, L1_cond_weight, L1_cond_mask, L1_cond_bias)
    x = x + _L2_cond_ref(x, cond_8, L2_cond_W_base, L2_cond_b_base, L2_cond_As, L2_cond_Bs)
    x = x + _L3_cond_ref(x, cond_8, L3_cond_W_up, L3_cond_b_up, L3_cond_W_gate, L3_cond_b_gate, L3_cond_W_down, L3_cond_b_down)
    return x

_drawn_inputs = setup_inputs


def setup_inputs(seed=0):
    import zlib

    import numpy as np

    out = dict(_drawn_inputs(seed))
    spreads = {'L3_cond_b_up': (0.0, 0.8), 'L3_cond_b_gate': (0.0, 0.8), 'L3_cond_b_down': (0.0, 0.1)}
    factors = {'L2_cond_b_base': 7.118}
    for name, (base, spread) in spreads.items():
        noise = np.random.default_rng([zlib.crc32(name.encode()), seed]).standard_normal(out[name].shape)
        drawn = base * np.exp(spread * noise) if base else spread * noise
        out[name] = jnp.asarray(drawn.astype(out[name].dtype))
    for name, factor in factors.items():
        out[name] = (out[name] * factor).astype(out[name].dtype)
    return out
```

```python
from contextlib import ExitStack

import concourse.bass as bass
from concourse import mybir

F32 = mybir.dt.float32
F32R = mybir.dt.float32r
I32 = mybir.dt.int32
ALU = mybir.AluOpType
ACT = mybir.ActivationFunctionType
AX = mybir.AxisListType

P = 128
NB, S, D = 64, 64, 256
E = 8
DC = D // P
I0, I3, R = 1024, 512, 16
NSH = NB // 2
NR0 = (2 * NB + E) // 2
G0 = NSH + NR0
G3 = (NB + E) // 2
SLOTS0, SLOTS3 = 2 * G0, 2 * G3
PIECE = 1024
NRAW = 3
HALF0 = 3 * PIECE
EXP0 = 2 * HALF0
EXP3 = 3 * PIECE
L1AT = EXP0
L2AT = L1AT + DC * E * D
NBIAS = 2 * I3 + D
NONE = NB
TOP_SCALE = 1.0 / 12
DMA_RING = 6144
STEP12 = 12 * (E + 1)
STEP3 = STEP12 + 10


def build(nc, x, xT, cond, w0, w1, mask, b1, w2, b2, w3, b3, out):
    with ExitStack() as ctx:
        def sb(name, shape, dt=F32):
            return ctx.enter_context(nc.sbuf_tensor(name, shape, dt))

        def sem(name):
            return ctx.enter_context(nc.semaphore(name))

        acc = sb("acc", [P, NB + 1, D])
        Wh = sb("Wh", [P, 2 * EXP0], F32R)
        Wl = sb("Wl", [P, 2 * EXP0], F32R)
        raw = sb("raw", [P, NRAW, PIECE])
        RS = sb("RS", [P, 3328], F32R)
        FS = sb("FS", [P, 3200])
        biases = sb("biases", [P, 2, NBIAS])
        b1s = sb("b1s", [P, D])
        b2s = sb("b2s", [P, D])
        ident = sb("ident", [P, P])
        one = sb("one", [P, 1])
        weight0 = sb("weight0", [P, G0])
        Y3 = sb("Y3", [P, E, G3])
        YT = sb("YT", [P, SLOTS3])
        batch0 = sb("batch0", [1, SLOTS0], I32)
        source0 = sb("source0", [1, SLOTS0], I32)
        expert0 = sb("expert0", [1, G0], I32)
        end0 = sb("end0", [1, E], I32)
        batch3 = sb("batch3", [1, SLOTS3], I32)
        dest3 = sb("dest3", [1, SLOTS3], I32)
        expert3 = sb("expert3", [1, G3], I32)
        end3 = sb("end3", [1, E], I32)

        xh = [RS[:, 512 * p:512 * p + 256] for p in range(2)]
        xl = [RS[:, 512 * p + 256:512 * p + 512] for p in range(2)]
        hh = [RS[:, 1024 + 1024 * h:1536 + 1024 * h] for h in range(2)]
        hl = [RS[:, 1536 + 1024 * h:2048 + 1024 * h] for h in range(2)]
        xraw = [FS[:, 256 * p:256 * p + 256] for p in range(2)]
        gl = [FS[:, 512 + 512 * h:1024 + 512 * h] for h in range(2)]
        hid = [FS[:, 1536 + 512 * h:2048 + 512 * h] for h in range(2)]
        x1h, x1l, x2h, x2l, x3h, x3l = (RS[:, 256 * k:256 * k + 256] for k in range(6))
        rh, rl = RS[:, 1536:1664], RS[:, 1664:1792]
        h3h, h3l = RS[:, 1792:2304], RS[:, 2304:2816]
        cross = FS[:, 0:256]
        x1 = [FS[:, 256:512], FS[:, 512:768]]
        x2, x2b, x3 = FS[:, 768:1024], FS[:, 1024:1280], FS[:, 1280:1536]
        x3d = [FS[:, 1536:1792], FS[:, 1792:2048]]
        up3, gate3 = FS[:, 2048:2560], FS[:, 2560:3072]
        ranks = FS[:, 3072:3200]

        rt = biases[:, :, :].rearrange("p a n -> p (a n)")
        iota_slot = rt[0:NB, 0:200]
        T0, T1, T2, TW = (rt[0:NB, 200 * k:200 * k + 200] for k in range(1, 5))
        T3 = rt[0:NB, 1000:1072]
        TY = rt[0:NB, 1072:1072 + E * SLOTS3].rearrange("b (e s) -> b e s", e=E)
        small = rt[0:NB, 1700:1700 + 400]
        tri = rt[0:NB, 2112:2112 + NB]
        ones = rt[0:NB, 2176:2176 + P]
        adapters = rt[0:NB, 2304:2304 + P]
        condt = rt[0:NB, 2432:2432 + E]
        maskt = FS[:, 2560:3072]
        passed = FS[0:1, 512:512 + E * G0].rearrange("p (g k) -> p g k", k=E)
        ended = FS[0:1, 1400:1400 + G0]

        bank = [ctx.enter_context(nc.psum_tensor(f"bank{k}", [P, 512], F32)) for k in range(8)]
        gate_ps, up_ps, turn_ps, out_ps = bank[0:2], bank[2:4], bank[4:6], bank[6:8]
        l1_ps, turnx_ps, low_ps, up3_ps, gate3_ps, turnh_ps, out3_ps = (
            bank[0:2], bank[2], bank[3], bank[4], bank[5], bank[6], bank[7])

        x_in_acc = sem("x_in_acc")
        cond_in = sem("cond_in")
        consts_made = sem("consts_made")
        zeros_made = sem("zeros_made")
        route_step = sem("route_step")
        route_max = sem("route_max")
        route_exp = sem("route_exp")
        route_masks = sem("route_masks")
        route_counts = sem("route_counts")
        route_slots = sem("route_slots")
        route_sums = sem("route_sums")
        tables_ready = sem("tables_ready")
        raw_in = [sem(f"raw_in{k}") for k in range(NRAW)]
        raw_free = sem("raw_free")
        slot_free = sem("slot_free")
        mask_in = sem("mask_in")
        masked = sem("masked")
        split_step = sem("split_step")
        bias_in = [sem(f"bias_in{k}") for k in range(2)]
        b12_in = sem("b12_in")
        xraw_in = [sem(f"xraw_in{p}") for p in range(2)]
        xh_done, xl_done = sem("xh_done"), sem("xl_done")
        gate_done, up_done = sem("gate_done"), sem("up_done")
        gelu_done, hid_done, turn_done = sem("gelu_done"), sem("hid_done"), sem("turn_done")
        hh_done, hl_done = sem("hh_done"), sem("hl_done")
        down_done, acc_done = sem("down_done"), sem("acc_done")
        cross_done, x1_done, t1_done = sem("cross_done"), sem("x1_done"), sem("t1_done")
        x1h_done, x1l_done = sem("x1h_done"), sem("x1l_done")
        l1_done, mix_step, mix_done = sem("l1_done"), sem("mix_step"), sem("mix_done")
        t2_done, x2h_done, x2l_done = sem("t2_done"), sem("x2h_done"), sem("x2l_done")
        low_done, ranks_done = sem("low_done"), sem("ranks_done")
        rh_done, rl_done, l2_done = sem("rh_done"), sem("rl_done"), sem("l2_done")
        x2b_done, x3_done, x3d_done = sem("x2b_done"), sem("x3_done"), sem("x3d_done")
        t3_done, x3h_done, x3l_done = sem("t3_done"), sem("x3h_done"), sem("x3l_done")
        up3_done, gate3_done = sem("up3_done"), sem("gate3_done")
        upb_done, silu_done, gateb_done = sem("upb_done"), sem("silu_done"), sem("gateb_done")
        hid3_done, turnh_done = sem("hid3_done"), sem("turnh_done")
        h3h_done, h3l_done = sem("h3h_done"), sem("h3l_done")
        down3_done = sem("down3_done")
        y_done = sem("y_done")
        out_done = [sem(f"out_done{p}") for p in range(2)]

        block = ctx.enter_context(nc.Block())

        @block.sync
        def _(sp):
            sp.dma_start(condt, cond).then_inc(cond_in, 16)
            xe = x.rearrange("(t j) s d -> j s t d", j=2)
            for j in range(2):
                sp.dma_start(acc[S * j:S * (j + 1), j:NB:2, :], xe[j]).then_inc(x_in_acc, 16)
            sp.dma_start(b1s[:, :], b1.rearrange("(a d) -> a d", a=1).broadcast_to([P, D])).then_inc(b12_in, 16)
            sp.dma_start(b2s[:, :], b2.rearrange("(a d) -> a d", a=1).broadcast_to([P, D])).then_inc(b12_in, 16)
            sp.wait_ge(tables_ready, 1)

            def load_x(g, p):
                for j in range(2):
                    b = sp.value_load(source0[0:1, bass.ds(2 * g + j, 1)], min_val=0, max_val=NB - 1)
                    dst = xraw[p].rearrange("p (c j s) -> p c j s", c=DC, j=2)[:, :, j, :]
                    sp.dma_start(dst, xT[bass.ds(b, 1)].rearrange("a p c s -> p (a c) s")).then_inc(xraw_in[p], 16)

            load_x(0, 0)
            load_x(1, 1)
            with sp.Fori(1, G0 // 2) as pair:
                g = 2 * pair
                for k in range(2):
                    sp.wait_ge(xl_done, g + k - 1)
                    load_x(g + k, k)

            def store(g, p):
                sp.wait_ge(y_done, g + 1)
                for j in range(2):
                    b = sp.value_load(dest3[0:1, bass.ds(2 * g + j, 1)], min_val=0, max_val=NB + SLOTS3 - 1)
                    sp.dma_start(out[bass.ds(b, 1)].rearrange("a s d -> (a s) d"),
                                 x3d[p][S * j:S * (j + 1), :]).then_inc(out_done[p], 16)

            with sp.Fori(0, G3 // 2) as pair:
                g = 2 * pair
                for k in range(2):
                    store(g + k, k)
            for p in range(2):
                sp.wait_ge(out_done[p], 32 * (G3 // 2))

        @block.gpsimd
        def _(pool):
            pool.iota(iota_slot, pattern=[[1, SLOTS0]], base=-NB, channel_multiplier=0,
                      allow_small_or_imprecise_dtypes=True)
            pool.iota(small[:, 0:E], pattern=[[1, E]], base=-E, channel_multiplier=0,
                      allow_small_or_imprecise_dtypes=True)
            pool.iota(small[:, 8:9], pattern=[[0, 1]], base=-NB, channel_multiplier=1,
                      allow_small_or_imprecise_dtypes=True)
            pool.memset(tri, 1.0)
            pool.memset(one[:, :], 1.0)
            pool.memset(ones, 1.0)
            pool.memset(ident[:, :], 0.0).then_inc(consts_made, 1)
            pool.wait_ge(consts_made, 1)
            pool.affine_select(out=tri, in_=tri, compare_op=ALU.is_gt, fill=0.0, base=0,
                               pattern=[[1, NB]], channel_multiplier=-1)
            pool.affine_select(out=ident[:, :], in_=ident[:, :], compare_op=ALU.not_equal, fill=1.0,
                               base=0, pattern=[[-1, P]], channel_multiplier=1).then_inc(consts_made, 1)

            def load(k, src):
                pool.dma_start(raw[:, k, :], src).then_inc(raw_in[k], 16)

            def split(k, step, at):
                hi, lo = Wh[:, at:at + PIECE], Wl[:, at:at + PIECE]
                pool.tensor_tensor(hi, raw[:, k, :], one[:, :].broadcast_to([P, PIECE]), ALU.mult).then_inc(split_step, 1)
                pool.wait_ge(split_step, step + 1)
                pool.tensor_tensor(lo, raw[:, k, :], hi.bitcast(F32), ALU.subtract).then_inc(split_step, 1)
                pool.wait_ge(split_step, step + 2)
                pool.sem_inc(raw_free, 1)

            def w0_piece(e, i):
                return w0[bass.ds(e, 1), :, i * PIECE:(i + 1) * PIECE].rearrange("a p n -> p (a n)")

            def expert(e, slot, last=False):
                for i in range(6):
                    k = i % NRAW
                    pool.wait_ge(raw_in[k], 32 * e + 16 * (i // NRAW) + 16)
                    split(k, 12 * e + 2 * i, slot * EXP0 + i * PIECE)
                    if i < NRAW:
                        load(k, w0_piece(e, i + NRAW))
                    elif not last:
                        load(k, w0_piece(e + 1, i - NRAW))

            def expert_in_ring(e, slot, last=False):
                end = pool.value_load(end0[0:1, bass.ds(e - 2, 1)], min_val=2 * NSH, max_val=2 * G0)
                pool.wait_ge(down_done, end)
                expert(e, slot, last)

            for i in range(NRAW):
                load(i, w0_piece(0, i))
            expert(0, 0)
            expert(1, 1)
            pool.wait_ge(tables_ready, 1)
            with pool.Fori(1, E // 2) as pair:
                e = 2 * pair
                expert_in_ring(e, 0)
                expert_in_ring(e + 1, 1)
            expert_in_ring(E, 0, last=True)

            arrived = [32 * (E + 1)] * NRAW
            srcs = [w1[:, n * PIECE:(n + 1) * PIECE] for n in range(4)] + [w2]
            pool.dma_start(maskt, mask).then_inc(mask_in, 16)
            for n in range(NRAW):
                load(n, srcs[n])
            pool.wait_ge(mask_in, 16)
            end = pool.value_load(end0[0:1, E - 1:E], min_val=2 * NSH, max_val=2 * G0)
            pool.wait_ge(down_done, end)
            for n in range(5):
                k = n % NRAW
                arrived[k] += 16
                pool.wait_ge(raw_in[k], arrived[k])
                if n < 4:
                    m = maskt[:, (n // 2) * D:(n // 2 + 1) * D].unsqueeze(1).broadcast_to([P, 4, D])
                    r4 = raw[:, k, :].rearrange("p (g o) -> p g o", g=4)
                    pool.tensor_tensor(r4, r4, m, ALU.mult).then_inc(masked, 1)
                    pool.wait_ge(masked, n + 1)
                split(k, STEP12 + 2 * n, L1AT + n * PIECE)
                if n + NRAW < 5:
                    load(k, srcs[n + NRAW])

            def w3_piece(e, m):
                return w3[bass.ds(e, 1), :, m * PIECE:(m + 1) * PIECE].rearrange("a p n -> p (a n)")

            def load_biases(e, slot):
                pool.dma_start(biases[:, slot, :], b3[bass.ds(e, 1), :].broadcast_to([P, NBIAS]))\
                    .then_inc(bias_in[slot], 16)

            def expert3_in(e, slot, last=False):
                pool.wait_ge(bias_in[slot], 8 * (e - slot) + 16)
                for m in range(3):
                    k = (2 + m) % NRAW
                    pool.wait_ge(raw_in[k], arrived[k] + 16 * e + 16)
                    split(k, STEP3 + 6 * e + 2 * m, slot * EXP3 + m * PIECE)
                    if not last:
                        load(k, w3_piece(e + 1, m))

            def expert3_in_ring(e, slot, last=False):
                end = pool.value_load(end3[0:1, bass.ds(e - 2, 1)], min_val=1, max_val=G3 + 1)
                pool.wait_ge(down3_done, end)
                pool.sem_inc(slot_free, 1)
                load_biases(e, slot)
                expert3_in(e, slot, last)

            for m in range(3):
                load((2 + m) % NRAW, w3_piece(0, m))
            load_biases(0, 0)
            load_biases(1, 1)
            pool.wait_ge(down_done, 2 * G0)
            expert3_in(0, 0)
            expert3_in(1, 1)
            with pool.Fori(1, (E - 2) // 2) as pair:
                e = 2 * pair
                expert3_in_ring(e, 0)
                expert3_in_ring(e + 1, 1)
            expert3_in_ring(E - 2, 0)
            expert3_in_ring(E - 1, 1, last=True)

        @block.tensor
        def _(pe):
            pe.wait_ge(consts_made, 2)
            pe.wait_ge(route_masks, 1)
            both = small[:, 64:80]
            pe.matmul(out_ps[0][0:NB, 0:16], tri, both, start=True, stop=True)
            pe.matmul(out_ps[1][0:NB, 0:16], ones[:, 0:NB], both, start=True, stop=True).then_inc(route_counts, 1)
            pe.wait_ge(route_slots, 1)
            colb = small[:, 8:9]
            pe.matmul(gate_ps[0][0:1, 0:SLOTS0], colb, T1, start=True, stop=True)
            pe.matmul(gate_ps[1][:, 0:SLOTS0], ones, TW, start=True, stop=True)
            pe.matmul(up_ps[0][0:1, 0:SLOTS3], colb, T3, start=True, stop=True)
            pe.matmul(up_ps[1][:, 0:SLOTS3], adapters, T3, start=True, stop=True)
            for q in range(2):
                mm = pe.matmul(turn_ps[q][:, 0:4 * SLOTS3], ones,
                               TY[:, 4 * q:4 * q + 4, :].rearrange("b e s -> b (e s)"), start=True, stop=True)
            mm.then_inc(route_sums, 1)
            pe.wait_ge(tables_ready, 1)

            def product(ps, pairs):
                n = len(pairs)
                for i, (ah, al, bh, bl) in enumerate(pairs):
                    pe.matmul(ps, ah, bh, start=(i == 0), stop=False)
                    pe.matmul(ps, ah, bl, start=False, stop=False)
                    mm = pe.matmul(ps, al, bh, start=False, stop=(i == n - 1))
                return mm

            def chunk(t, c):
                return t[:, c * P:(c + 1) * P]

            def weights(at, n):
                return Wh[:, bass.ds(at, n)], Wl[:, bass.ds(at, n)]

            def load_expert(g):
                return pe.value_load(expert0[0:1, bass.ds(g, 1)], min_val=0, max_val=E)

            def up_gate(g, p, h, e, n2, first=False):
                at = (e % 2) * EXP0 + h * HALF0
                if h == 0:
                    pe.wait_ge(xl_done, g + 1)
                pe.wait_ge(split_step, 12 * e + 6 * h + 4)
                if not first:
                    pe.wait_ge(hid_done, n2 - 1)
                product(gate_ps[h][:, :], [(chunk(xh[p], c), chunk(xl[p], c), *weights(at + c * 512, 512))
                                           for c in range(DC)]).then_inc(gate_done, 1)
                product(up_ps[h][:, :], [(chunk(xh[p], c), chunk(xl[p], c), *weights(at + PIECE + c * 512, 512))
                                         for c in range(DC)]).then_inc(up_done, 1)

            def turn(h, n2, first=False):
                pe.wait_ge(hid_done, n2 + 1)
                if not first:
                    pe.wait_ge(hl_done, n2 - 1)
                for c in range(4):
                    mm = pe.transpose(chunk(turn_ps[h], c), chunk(hid[h], c), ident[:, :])
                mm.then_inc(turn_done, 1)

            def down(g, p, h, e, n2, first=False):
                at = (e % 2) * EXP0 + h * HALF0 + 2 * PIECE
                pe.wait_ge(hl_done, n2 + 1)
                pe.wait_ge(split_step, 12 * e + 6 * h + 6)
                if h == 0 and not first:
                    pe.wait_ge(acc_done, g - 1)
                ps = out_ps[p][:, 0:D]
                for c in range(4):
                    wh, wl = weights(at + c * D, D)
                    pe.matmul(ps, chunk(hh[h], c), wh, start=(h == 0 and c == 0), stop=False)
                    pe.matmul(ps, chunk(hh[h], c), wl, start=False, stop=False)
                    mm = pe.matmul(ps, chunk(hl[h], c), wh, start=False, stop=(h == 1 and c == 3))
                mm.then_inc(down_done, 1)

            def group(g, p, n=3):
                e = load_expert(g)
                up_gate(g, p, 0, e, 2 * g, first=n < 1)
                if n > 0:
                    before = load_expert(g - 1)
                    turn(1, 2 * g - 1, first=n < 2)
                    down(g - 1, 1 - p, 0, before, 2 * g - 2, first=n < 3)
                up_gate(g, p, 1, e, 2 * g + 1, first=n < 1)
                turn(0, 2 * g, first=n < 1)
                if n > 0:
                    down(g - 1, 1 - p, 1, before, 2 * g - 1, first=n < 3)

            for g in range(3):
                group(g, g % 2, n=g)
            group(3, 1)
            with pe.Fori(2, G0 // 2) as pair:
                g = 2 * pair
                group(g, 0)
                group(g + 1, 1)
            last = load_expert(G0 - 1)
            turn(1, 2 * G0 - 1)
            down(G0 - 1, 1, 0, last, 2 * G0 - 2)
            down(G0 - 1, 1, 1, last, 2 * G0 - 1)

            def turn_x(t, ps):
                for c in range(DC):
                    mm = pe.transpose(chunk(ps, c), chunk(t, c), ident[:, :])
                return mm

            def turn_x1(i, p, first=False):
                pe.wait_ge(x1_done, i + 1)
                if first:
                    pe.wait_ge(hl_done, 2 * G0)
                    pe.wait_ge(acc_done, G0)
                else:
                    pe.wait_ge(h3l_done, i - 2)
                return turn_x(x1[p], turnh_ps)

            def layer1(i, k, first=False):
                if k == 0:
                    pe.wait_ge(x1l_done, i + 1)
                if not (first and k < 2):
                    pe.wait_ge(mix_done, 4 * i + k - 1)
                product(l1_ps[k % 2][:, :], [(chunk(x1h, c), chunk(x1l, c),
                                              Wh[:, L1AT + c * E * D + k * 512:L1AT + c * E * D + (k + 1) * 512],
                                              Wl[:, L1AT + c * E * D + k * 512:L1AT + c * E * D + (k + 1) * 512])
                                             for c in range(DC)]).then_inc(l1_done, 1)

            def low(i, first=False):
                pe.wait_ge(x2l_done, i + 1)
                if not first:
                    pe.wait_ge(x3_done, i)
                at = L2AT + 2 * D
                product(low_ps[:, 0:P], [(Wh[:, at + c * P:at + (c + 1) * P], Wl[:, at + c * P:at + (c + 1) * P],
                                          chunk(x2h, c), chunk(x2l, c)) for c in range(DC)]).then_inc(low_done, 1)

            def layer2(i):
                pe.wait_ge(rl_done, i + 1)
                pairs = [(chunk(x2h, c), chunk(x2l, c), Wh[:, L2AT + c * D:L2AT + (c + 1) * D],
                          Wl[:, L2AT + c * D:L2AT + (c + 1) * D]) for c in range(DC)]
                at = L2AT + 3 * D
                pairs.append((rh, rl, Wh[:, at:at + D], Wl[:, at:at + D]))
                product(low_ps[:, P:P + D], pairs).then_inc(l2_done, 1)

            def turn_x2(i, first=False):
                pe.wait_ge(mix_done, 4 * i + 4)
                if not first:
                    pe.wait_ge(x3l_done, i)
                turn_x(x2, turnx_ps).then_inc(t2_done, 1)

            def turn_x3(i):
                pe.wait_ge(x3_done, i + 1)
                pe.wait_ge(x2l_done, i + 1)
                turn_x(x3, turnx_ps).then_inc(t3_done, 1)

            def load_expert3(i):
                return pe.value_load(expert3[0:1, bass.ds(i, 1)], min_val=0, max_val=E - 1)

            def up_gate3(i, first=False):
                e = load_expert3(i)
                at = (e % 2) * EXP3
                pe.wait_ge(x3l_done, i + 1)
                pe.wait_ge(split_step, STEP3 + 6 * e + 4)
                if not first:
                    pe.wait_ge(hid3_done, i)
                for ps, k, done in ((up3_ps, 0, up3_done), (gate3_ps, 1, gate3_done)):
                    product(ps[:, :], [(chunk(x3h, c), chunk(x3l, c), *weights(at + k * PIECE + c * 512, 512))
                                       for c in range(DC)]).then_inc(done, 1)

            def turn_h(i):
                pe.wait_ge(hid3_done, i + 1)
                pe.wait_ge(x1l_done, min(i + 3, G3) if isinstance(i, int) else i + 3)
                for c in range(4):
                    mm = pe.transpose(chunk(turnh_ps, c), chunk(gate3, c), ident[:, :])
                mm.then_inc(turnh_done, 1)

            def down3(i, first=False):
                e = load_expert3(i)
                at = (e % 2) * EXP3 + 2 * PIECE
                pe.wait_ge(h3l_done, i + 1)
                pe.wait_ge(split_step, STEP3 + 6 * e + 6)
                if not first:
                    pe.wait_ge(y_done, i)
                product(out3_ps[:, 0:D], [(chunk(h3h, c), chunk(h3l, c), *weights(at + c * D, D))
                                          for c in range(4)]).then_inc(down3_done, 1)

            turn_x1(0, 0, first=True).then_inc(t1_done, 1)
            pe.sem_inc(down3_done, 1)
            pe.wait_ge(split_step, STEP3)

            def step(i, p, now=True, one=True, two=True, after=True, first=False, second=False, third=False):
                if now:
                    layer1(i, 0, first=first)
                if one:
                    low(i - 1, first=second)
                if two:
                    turn_h(i - 2)
                if now:
                    layer1(i, 1, first=first)
                if one:
                    layer2(i - 1)
                if now:
                    layer1(i, 2)
                if one:
                    turn_x3(i - 1)
                if two:
                    down3(i - 2, first=third)
                if now:
                    layer1(i, 3)
                if after:
                    turn_x1(i + 1, 1 - p, first=first or second).then_inc(t1_done, 1)
                if one:
                    up_gate3(i - 1, first=second)
                if now:
                    turn_x2(i, first=first)

            step(0, 0, one=False, two=False, first=True)
            step(1, 1, two=False, second=True)
            step(2, 0, third=True)
            step(3, 1)
            with pe.Fori(2, (G3 - 2) // 2) as pair:
                i = 2 * pair
                step(i, 0)
                step(i + 1, 1)
            step(G3 - 2, 0)
            step(G3 - 1, 1, after=False)
            step(G3, 0, now=False, after=False)
            step(G3 + 1, 1, now=False, one=False, after=False)

        @block.scalar
        def _(act):
            act.wait_ge(route_max, 1)
            act.activation(small[:, 32:40], condt, ACT.Exp, bias=small[:, 17:18],
                           accum_out=small[:, 18:19]).then_inc(route_exp, 1)

            def split_x(g, p, first=False):
                act.wait_ge(xraw_in[p], 32 * (g // 2) + 32 if isinstance(g, int) else 16 * (g - p) + 32)
                if not first:
                    act.wait_ge(up_done, 2 * g - 2)
                act.activation(xh[p], xraw[p], ACT.Copy).then_inc(xh_done, 1)

            def gelu(h, n2, first=False):
                act.wait_ge(gate_done, n2 + 1)
                if not first:
                    act.wait_ge(hid_done, n2 - 1)
                act.activation(gl[h], gate_ps[h][:, :], ACT.Gelu_apprx_tanh).then_inc(gelu_done, 1)

            def hidden_hi(h, n2, first=False):
                act.wait_ge(turn_done, n2 + 1)
                if not first:
                    act.wait_ge(down_done, n2 - 1)
                act.activation(hh[h], turn_ps[h][:, :], ACT.Copy).then_inc(hh_done, 1)

            def group(g, p, n=3, after=True):
                gelu(0, 2 * g, first=n < 1)
                if n > 0:
                    hidden_hi(1, 2 * g - 1, first=n < 2)
                if after:
                    split_x(g + 1, 1 - p, first=n < 1)
                gelu(1, 2 * g + 1, first=n < 1)
                hidden_hi(0, 2 * g, first=n < 1)

            act.wait_ge(tables_ready, 1)
            split_x(0, 0, first=True)
            group(0, 0, n=0)
            group(1, 1, n=1)
            with act.Fori(1, (G0 - 2) // 2) as pair:
                g = 2 * pair
                group(g, 0)
                group(g + 1, 1)
            group(G0 - 2, 0)
            group(G0 - 1, 1, after=False)
            hidden_hi(1, 2 * G0 - 1)

            def cross_over(i, first=False):
                if first:
                    act.wait_ge(acc_done, G0)
                else:
                    act.wait_ge(x1_done, i)
                for j in range(2):
                    b = act.value_load(batch3[0:1, bass.ds(2 * i + j, 1)], min_val=0, max_val=NONE)
                    op = act.activation(cross[S * j:S * (j + 1), :],
                                        acc[S * (1 - j):S * (2 - j), bass.ds(b, 1), :].rearrange("p a d -> p (a d)"),
                                        ACT.Copy)
                op.then_inc(cross_done, 1)

            def hi(arrived, count, dst, src, done, free=None, freed=None):
                act.wait_ge(arrived, count)
                if free is not None:
                    act.wait_ge(free, freed)
                act.activation(dst, src, ACT.Copy).then_inc(done, 1)

            def silu(i):
                act.wait_ge(upb_done, i + 1)
                act.activation(up3, up3, ACT.Silu).then_inc(silu_done, 1)

            def step(i, now=True, one=True, two=True, after=True, after2=True, first=False, second=False, third=False):
                if one:
                    hi(ranks_done, i, rh, ranks, rh_done, *((None, None) if second else (l2_done, i - 1)))
                if two:
                    hi(turnh_done, i - 1, h3h, turnh_ps[:, :], h3h_done,
                       *((None, None) if third else (down3_done, i - 1)))
                if one:
                    hi(t3_done, i, x3h, turnx_ps[:, 0:D], x3h_done, *((None, None) if second else (gate3_done, i - 1)))
                if after:
                    hi(t1_done, i + 2, x1h, turnh_ps[:, 0:D], x1h_done, l1_done, 4 * i + 4)
                if one:
                    silu(i - 1)
                if now:
                    hi(t2_done, i + 1, x2h, turnx_ps[:, 0:D], x2h_done, *((None, None) if first else (l2_done, i)))
                if after2:
                    cross_over(i + 2)

            cross_over(0, first=True)
            cross_over(1)
            hi(t1_done, 1, x1h, turnh_ps[:, 0:D], x1h_done)
            step(0, one=False, two=False, first=True)
            step(1, two=False, second=True)
            step(2, third=True)
            step(3)
            with act.Fori(2, (G3 - 2) // 2) as pair:
                i = 2 * pair
                step(i)
                step(i + 1)
            step(G3 - 2, after2=False)
            step(G3 - 1, after=False, after2=False)
            step(G3, now=False, after=False, after2=False)
            step(G3 + 1, now=False, one=False, after=False, after2=False)

        @block.vector
        def _(dve):
            dve.memset(acc[0:S, 1:NB:2, :], 0.0)
            dve.memset(acc[S:P, 0:NB:2, :], 0.0)
            dve.memset(acc[:, NONE, :], 0.0).then_inc(zeros_made, 1)

            count = [0]

            def done(op):
                count[0] += 1
                op.then_inc(route_step, 1)
                dve.wait_ge(route_step, count[0])

            TT, TS, STT = dve.tensor_tensor, dve.tensor_scalar, dve.scalar_tensor_tensor
            eid = small[:, 0:E]
            colb = small[:, 8:9]
            def col(k):
                return small[:, k:k + 1]
            m1, i1, m2, i2, nm1, ssum, w1c, w2c, rc, pos1, pos2, pos3 = (
                col(k) for k in (16, 19, 20, 21, 17, 18, 22, 23, 24, 25, 26, 27))
            ex, junk = small[:, 32:40], small[:, 40:48]
            M1, M2 = small[:, 48:56], small[:, 56:64]
            both = small[:, 64:80].rearrange("b (a e) -> b a e", a=2)
            Mt, M3 = both[:, 0, :], both[:, 1, :]
            cond2 = small[:, 80:88]

            dve.wait_ge(cond_in, 16)
            dve.wait_ge(consts_made, 2)
            done(dve.tensor_reduce(m1, condt, AX.X, ALU.max))
            TS(nm1, m1, -1.0, None, ALU.mult).then_inc(route_max, 1)

            def first_of(values, top, index, mask):
                done(TS(junk, values, top, None, ALU.is_ge))
                done(TT(junk, junk, eid, ALU.mult))
                done(dve.tensor_reduce(index, junk, AX.X, ALU.min))
                done(TS(mask, eid, index, None, ALU.is_equal))

            first_of(condt, m1, i1, M1)
            done(STT(cond2, M1, -3.0e38, condt, ALU.mult, ALU.add))
            done(dve.tensor_reduce(m2, cond2, AX.X, ALU.max))
            first_of(cond2, m2, i2, M2)
            TT(Mt, M1, M2, ALU.add)
            dve.tensor_copy(M3, M1).then_inc(route_masks, 1)

            dve.wait_ge(route_exp, 1)
            done(dve.reciprocal(rc, ssum))
            done(TS(ex, ex, rc, None, ALU.mult))
            for m, w in ((M1, w1c), (M2, w2c)):
                done(TT(junk, ex, m, ALU.mult))
                done(dve.tensor_reduce(w, junk, AX.X, ALU.add))
            done(TT(rc, w1c, w2c, ALU.add))
            done(dve.reciprocal(rc, rc))
            for w in (w1c, w2c):
                done(TT(w, w, rc, ALU.mult))
                done(TS(col(28), w, TOP_SCALE, None, ALU.mult))
                done(STT(w, w, 1.0 - TOP_SCALE, col(28), ALU.mult, ALU.add))

            ints = small[:, 88:104].bitcast(I32)
            def three(k):
                return small[:, k:k + 16].rearrange("b (a e) -> b a e", a=2)
            groups, sum1, sum2, ends, begins = three(104), three(120), three(136), three(152), three(168)
            places = three(184)
            dve.wait_ge(route_counts, 1)
            done(TS(ints, out_ps[1][0:NB, 0:16], 1.0, None, ALU.add))
            done(TS(ints, ints, 1, None, ALU.logical_shift_right))
            done(dve.tensor_copy(groups, ints.rearrange("b (a e) -> b a e", a=2)))
            for a, b, k in ((groups, sum1, 1), (sum1, sum2, 2), (sum2, ends, 4)):
                dve.tensor_copy(b[:, :, 0:k], a[:, :, 0:k])
                done(TT(b[:, :, k:E], a[:, :, k:E], a[:, :, 0:E - k], ALU.add))
            done(TT(begins, ends, groups, ALU.subtract))
            ranks_ps = out_ps[0][0:NB, 0:16].rearrange("b (a e) -> b a e", a=2)
            done(STT(places, begins, 2.0, ranks_ps, ALU.mult, ALU.add))
            for m, a, pos in ((M1, 0, pos1), (M2, 0, pos2), (M1, 1, pos3)):
                done(TT(junk, places[:, a, :], m, ALU.mult))
                done(dve.tensor_reduce(pos, junk, AX.X, ALU.add))

            TS(T0, iota_slot, colb, None, ALU.is_equal)
            TS(T1, iota_slot, pos1, None, ALU.is_equal)
            TS(T3, iota_slot[:, NB:NB + SLOTS3], pos3, None, ALU.is_equal)
            done(TS(T2, iota_slot, pos2, None, ALU.is_equal))
            done(STT(TW, T1, w1c, T0, ALU.mult, ALU.add))
            done(STT(TW, T2, w2c, TW, ALU.mult, ALU.add))
            done(TT(T1, T1, T0, ALU.add))
            done(TT(T1, T1, T2, ALU.add))
            TT(TY, T3.unsqueeze(1).broadcast_to([NB, E, SLOTS3]),
               condt.unsqueeze(2).broadcast_to([NB, E, SLOTS3]), ALU.mult)
            TS(adapters.rearrange("b (e r) -> b e r", e=E), condt.unsqueeze(2).broadcast_to([NB, E, R]),
               2.0, None, ALU.mult).then_inc(route_slots, 1)

            row = small[0:1, 200:208]
            for a, n, table, table_end in ((0, G0, expert0, end0), (1, G3, expert3, end3)):
                if a == 0:
                    dve.memset(row[:, 0:1], float(NSH))
                    done(TS(row[:, 1:E], ends[0:1, 0, 0:E - 1], float(NSH), None, ALU.add))
                    done(TS(table_end[:, :], row, 2.0, None, ALU.mult))
                    iota_group = iota_slot[0:1, NB:NB + G0]
                    used = E
                else:
                    done(dve.tensor_copy(row, ends[0:1, 1, :]))
                    done(TS(table_end[:, :], row, 1.0, None, ALU.add))
                    iota_group = iota_slot[0:1, NB:NB + G3]
                    used = E - 1
                v = passed[:, 0:n, 0:used]
                done(TT(v, iota_group.unsqueeze(2).broadcast_to([1, n, used]),
                        row[:, 0:used].unsqueeze(1).broadcast_to([1, n, used]), ALU.is_ge))
                done(dve.tensor_reduce(ended[:, 0:n], v, AX.X, ALU.add))
                done(dve.tensor_copy(table[:, :], ended[:, 0:n]))

            dve.wait_ge(route_sums, 1)
            done(TS(batch0[:, :], gate_ps[0][0:1, 0:SLOTS0], float(NONE), None, ALU.add))
            done(TS(source0[:, :], batch0[:, :], float(NB - 1), None, ALU.min))
            for j in range(2):
                half = slice(S * j, S * (j + 1))
                dve.tensor_copy(weight0[half, :], gate_ps[1][half, j:SLOTS0:2])
                for q in range(2):
                    dve.tensor_copy(Y3[half, 4 * q:4 * q + 4, :],
                                    turn_ps[q][half, 0:4 * SLOTS3].rearrange("p (e g j) -> p e g j", e=4, j=2)[:, :, :, j])
            dve.tensor_copy(YT[:, :], up_ps[1][:, 0:SLOTS3])
            done(TS(batch3[:, :], up_ps[0][0:1, 0:SLOTS3], float(NONE), None, ALU.add))
            none3 = passed[:, :, :].rearrange("p g k -> p (g k)")[:, 0:SLOTS3]
            done(TS(none3, batch3[:, :], float(NONE), None, ALU.is_equal))
            done(TT(none3, none3, iota_slot[0:1, NB:NB + SLOTS3], ALU.mult))
            done(TT(dest3[:, :], batch3[:, :], none3, ALU.add))
            dve.nop().then_inc(tables_ready, 1)

            def split_x(g, p):
                dve.wait_ge(xh_done, g + 1)
                TT(xl[p], xraw[p], xh[p].bitcast(F32), ALU.subtract).then_inc(xl_done, 1)

            def hidden(h, n2, first=False):
                dve.wait_ge(gelu_done, n2 + 1)
                dve.wait_ge(up_done, n2 + 1)
                if not first:
                    dve.wait_ge(turn_done, n2 - 1)
                TT(hid[h], up_ps[h][:, :], gl[h], ALU.mult).then_inc(hid_done, 1)

            def hidden_lo(h, n2):
                dve.wait_ge(hh_done, n2 + 1)
                TT(hl[h], turn_ps[h][:, :], hh[h].bitcast(F32), ALU.subtract).then_inc(hl_done, 1)

            def add(g, p, first=False):
                dve.wait_ge(down_done, 2 * g + 2)
                if not first:
                    dve.wait_ge(acc_done, g)
                for j in range(2):
                    b = dve.value_load(batch0[0:1, bass.ds(2 * g + j, 1)], min_val=0, max_val=NONE)
                    half = slice(S * j, S * (j + 1))
                    at = acc[half, bass.ds(b, 1), :].rearrange("p a d -> p (a d)")
                    op = STT(at, out_ps[p][half, 0:D], weight0[half, bass.ds(g, 1)], at, ALU.mult, ALU.add)
                op.then_inc(acc_done, 1)

            def group(g, p, n=3, after=True):
                hidden(0, 2 * g, first=n < 1)
                if n > 0:
                    hidden_lo(1, 2 * g - 1)
                if after:
                    split_x(g + 1, 1 - p)
                hidden(1, 2 * g + 1, first=n < 1)
                hidden_lo(0, 2 * g)
                if n > 0:
                    add(g - 1, 1 - p, first=n < 2)

            split_x(0, 0)
            group(0, 0, n=0)
            dve.wait_ge(zeros_made, 1)
            dve.wait_ge(x_in_acc, 32)
            group(1, 1, n=1)
            with dve.Fori(1, (G0 - 2) // 2) as pair:
                g = 2 * pair
                group(g, 0)
                group(g + 1, 1)
            group(G0 - 2, 0)
            group(G0 - 1, 1, after=False)
            hidden_lo(1, 2 * G0 - 1)
            add(G0 - 1, 1)

            def join(i, p, first=False):
                dve.wait_ge(cross_done, i + 1)
                if first:
                    dve.wait_ge(acc_done, G0)
                else:
                    dve.wait_ge(t1_done, i - 1)
                for j in range(2):
                    b = dve.value_load(batch3[0:1, bass.ds(2 * i + j, 1)], min_val=0, max_val=NONE)
                    half = slice(S * j, S * (j + 1))
                    op = TT(x1[p][half, :], cross[half, :], acc[half, bass.ds(b, 1), :].rearrange("p a d -> p (a d)"),
                            ALU.add)
                op.then_inc(x1_done, 1)

            def mix(i, p, k, first=False):
                if k == 0:
                    dve.wait_ge(x1_done, i + 1)
                    if not first:
                        dve.wait_ge(t2_done, i)
                        dve.wait_ge(x2b_done, i)
                    TT(x2, x1[p], b1s[:, :], ALU.add).then_inc(mix_step, 1)
                dve.wait_ge(l1_done, 4 * i + k + 1)
                for q in range(2):
                    dve.wait_ge(mix_step, 9 * i + 2 * k + q + 1)
                    op = STT(x2, l1_ps[k % 2][:, q * D:(q + 1) * D],
                             Y3[:, 2 * k + q, bass.ds(i, 1)], x2, ALU.mult, ALU.add)
                    op.then_inc(mix_step, 1)
                    if q == 1:
                        dve.wait_ge(mix_step, 9 * i + 2 * k + q + 2)
                        dve.sem_inc(mix_done, 1)

            def lo(i, dst, src, hi, hi_done, done_):
                dve.wait_ge(hi_done, i)
                TT(dst, src, hi.bitcast(F32), ALU.subtract).then_inc(done_, 1)

            def weigh(i):
                dve.wait_ge(low_done, i + 1)
                for j in range(2):
                    op = TS(ranks[:, S * j:S * (j + 1)], low_ps[:, S * j:S * (j + 1)],
                            YT[:, bass.ds(2 * i + j, 1)], None, ALU.mult)
                op.then_inc(ranks_done, 1)

            def finish2(i, p, first=False):
                dve.wait_ge(l2_done, i + 1)
                dve.wait_ge(x2b_done, i + 1)
                if not first:
                    dve.wait_ge(t3_done, i)
                    dve.wait_ge(x3d_done, i)
                TT(x3, low_ps[:, P:P + D], x2b, ALU.add).then_inc(x3_done, 1)

            def finish2b(i, p, early=False):
                e = dve.value_load(expert3[0:1, bass.ds(i, 1)], min_val=0, max_val=E - 1)
                dve.wait_ge(x3_done, i + 1)
                dve.wait_ge(split_step, STEP3 + 6 * e + 2)
                if not early:
                    dve.wait_ge(out_done[p], 16 * (i - p))
                TT(x3d[p], x3, biases[:, bass.ds(e % 2, 1), 2 * I3:NBIAS].rearrange("p a n -> p (a n)"),
                   ALU.add).then_inc(x3d_done, 1)

            def hidden3(i, first=False):
                e = dve.value_load(expert3[0:1, bass.ds(i, 1)], min_val=0, max_val=E - 1)
                def bias(k):
                    return biases[:, bass.ds(e % 2, 1), k * I3:(k + 1) * I3].rearrange("p a n -> p (a n)")
                dve.wait_ge(up3_done, i + 1)
                if not first:
                    dve.wait_ge(hid3_done, i)
                    dve.wait_ge(turnh_done, i)
                TT(up3, up3_ps[:, :], bias(0), ALU.add).then_inc(upb_done, 1)
                dve.wait_ge(gate3_done, i + 1)
                TT(gate3, gate3_ps[:, :], bias(1), ALU.add).then_inc(gateb_done, 1)
                dve.wait_ge(silu_done, i + 1)
                dve.wait_ge(gateb_done, i + 1)
                TT(gate3, up3, gate3, ALU.mult).then_inc(hid3_done, 1)

            def finish3(i, p):
                dve.wait_ge(down3_done, i + 2)
                dve.wait_ge(x3d_done, i + 1)
                TT(x3d[p], out3_ps[:, 0:D], x3d[p], ALU.add).then_inc(y_done, 1)

            def step(i, p, now=True, one=True, two=True, after=True, first=False, second=False, early=False):
                if after:
                    join(i + 1, 1 - p, first=first)
                if now:
                    mix(i, p, 0, first=first)
                if one:
                    weigh(i - 1)
                    dve.wait_ge(ranks_done, i)
                    lo(i, rl, ranks, rh, rh_done, rl_done)
                if two:
                    lo(i - 1, h3l, turnh_ps[:, :], h3h, h3h_done, h3l_done)
                if now:
                    mix(i, p, 1)
                if one:
                    finish2(i - 1, 1 - p, first=second)
                if now:
                    mix(i, p, 2)
                if one:
                    lo(i, x3l, turnx_ps[:, 0:D], x3h, x3h_done, x3l_done)
                    finish2b(i - 1, 1 - p, early=early)
                if two:
                    finish3(i - 2, p)
                if now:
                    mix(i, p, 3)
                    if not first:
                        dve.wait_ge(x3_done, i)
                    TT(x2b, x2, b2s[:, :], ALU.add).then_inc(x2b_done, 1)
                if after:
                    lo(i + 2, x1l, turnh_ps[:, 0:D], x1h, x1h_done, x1l_done)
                if one:
                    hidden3(i - 1, first=second)
                if now:
                    lo(i + 1, x2l, turnx_ps[:, 0:D], x2h, x2h_done, x2l_done)

            dve.wait_ge(b12_in, 32)
            join(0, 0, first=True)
            lo(1, x1l, turnh_ps[:, 0:D], x1h, x1h_done, x1l_done)
            step(0, 0, one=False, two=False, first=True)
            step(1, 1, two=False, second=True, early=True)
            step(2, 0, early=True)
            step(3, 1)
            with dve.Fori(2, (G3 - 2) // 2) as pair:
                i = 2 * pair
                step(i, 0)
                step(i + 1, 1)
            step(G3 - 2, 0)
            step(G3 - 1, 1, after=False)
            step(G3, 0, now=False, after=False)
            step(G3 + 1, 1, now=False, one=False, after=False)


def kernel(x, cond_8, L0_cond_skill_gate, L0_cond_skill_up, L0_cond_skill_down, L0_cond_shared_gate,
           L0_cond_shared_up, L0_cond_shared_down, L1_cond_weight, L1_cond_mask, L1_cond_bias,
           L2_cond_W_base, L2_cond_b_base, L2_cond_As, L2_cond_Bs, L3_cond_W_up, L3_cond_b_up,
           L3_cond_W_gate, L3_cond_b_gate, L3_cond_W_down, L3_cond_b_down):
    import numpy as np

    import concourse.bacc as bacc
    from concourse.bass_utils import run_bass_kernel_spmd

    def rows(w):
        w = np.asarray(w)
        return np.swapaxes(w.reshape(*w.shape[:-2], w.shape[-2] // P, P, w.shape[-1]), -3, -2)

    x = np.asarray(x)
    gate = rows(np.concatenate([np.asarray(L0_cond_shared_gate)[None], np.asarray(L0_cond_skill_gate)]))
    up = rows(np.concatenate([np.asarray(L0_cond_shared_up)[None], np.asarray(L0_cond_skill_up)]))
    down = rows(np.concatenate([np.asarray(L0_cond_shared_down)[None], np.asarray(L0_cond_skill_down)]))
    parts = []
    for h in range(2):
        parts += [gate[..., 512 * h:512 * (h + 1)].reshape(E + 1, P, PIECE),
                  up[..., 512 * h:512 * (h + 1)].reshape(E + 1, P, PIECE),
                  down[:, :, 4 * h:4 * (h + 1)].reshape(E + 1, P, PIECE)]
    w1 = np.swapaxes(rows(np.swapaxes(np.asarray(L1_cond_weight), 1, 2)), 0, 1)
    w1 = np.swapaxes(w1, 1, 2).reshape(P, DC * E * D)
    mask = rows(np.asarray(L1_cond_mask).T).reshape(P, DC * D)
    w2 = np.concatenate([rows(np.asarray(L2_cond_W_base).T).reshape(P, DC * D),
                         rows(np.asarray(L2_cond_As).reshape(E * R, D).T).reshape(P, DC * E * R),
                         np.swapaxes(np.asarray(L2_cond_Bs), 1, 2).reshape(E * R, D)], axis=1)
    w3 = np.concatenate([rows(np.swapaxes(np.asarray(w), 1, 2)).reshape(E, P, PIECE)
                         for w in (L3_cond_W_up, L3_cond_W_gate, L3_cond_W_down)], axis=2)
    b3 = np.concatenate([np.asarray(b) for b in (L3_cond_b_up, L3_cond_b_gate, L3_cond_b_down)], axis=1)
    ins = {
        "x": x,
        "xT": rows(np.swapaxes(x, 1, 2)),
        "cond": np.asarray(cond_8),
        "w0": np.concatenate(parts, axis=2),
        "w1": w1, "mask": mask, "b1": np.asarray(L1_cond_bias),
        "w2": w2, "b2": np.asarray(L2_cond_b_base),
        "w3": w3, "b3": b3,
    }
    ins = {k: np.ascontiguousarray(v) for k, v in ins.items()}
    nc = bacc.Bacc("TRN2", target_bir_lowering=False, num_devices=1, dynamic_dma_scratch_size=DMA_RING)
    aps = {k: nc.dram_tensor(f"in_{k}", v.shape, mybir.dt.from_np(v.dtype), kind="ExternalInput").ap()
           for k, v in ins.items()}
    out = nc.dram_tensor("out_rows", (NB + SLOTS3, S, D), F32, kind="ExternalOutput").ap()
    build(nc, **aps, out=out)
    result = run_bass_kernel_spmd(nc, [{f"in_{k}": v for k, v in ins.items()}], core_ids=[0])
    return result.results[0]["out_rows"][:NB]
```

```python
from contextlib import ExitStack

import concourse.bass as bass
from concourse import mybir

F32 = mybir.dt.float32
F32R = mybir.dt.float32r
I32 = mybir.dt.int32
ALU = mybir.AluOpType
ACT = mybir.ActivationFunctionType
AX = mybir.AxisListType

P = 128
NB, S, D = 64, 64, 256
E = 8
DC = D // P
I0, I3, R = 1024, 512, 16
NSH = NB // 2
NR0 = (2 * NB + E) // 2
G0 = NSH + NR0
G3 = (NB + E) // 2
SLOTS0, SLOTS3 = 2 * NR0, 2 * G3
SLOTS = SLOTS0 + SLOTS3
PIECE = 1024
NRAW = 3
HALF0 = 3 * PIECE
EXP0 = 2 * HALF0
EXP3 = 3 * PIECE
L1AT = EXP0
L2AT = L1AT + DC * E * D
NBIAS = 2 * I3 + 2 * D
BIASAT = NSH + EXP0 // D
NONE = NB
TOP_SCALE = 1.0 / 12
DMA_RING = 6144
STEP12 = 12 * E
STEP3 = STEP12 + 10


def build(nc, x, xT, cond, condT, w0, w1, mask, b1, w2, b2, w3, b3, out):
    with ExitStack() as ctx:
        def sb(name, shape, dt=F32):
            return ctx.enter_context(nc.sbuf_tensor(name, shape, dt))

        def sem(name):
            return ctx.enter_context(nc.semaphore(name))

        acc = sb("acc", [P, NB + 1, D])
        Wh = sb("Wh", [P, 2 * EXP0], F32R)
        Wl = sb("Wl", [P, 2 * EXP0], F32R)
        raw = sb("raw", [P, NRAW, PIECE])
        RS = sb("RS", [P, 3072], F32R)
        FS = sb("FS", [P, 2560])
        routing = sb("routing", [P, 1720])
        rows3 = sb("rows3", [64, NBIAS], F32R)
        pick2 = sb("pick2", [64, P], F32R)
        pick3 = sb("pick3", [64, 2, P], F32R)
        b1s = sb("b1s", [P, D])
        ident = sb("ident", [P, P])
        one = sb("one", [P, 1])
        weight0 = sb("weight0", [P, NR0])
        Y1 = sb("Y1", [P, NSH, E])
        YT = sb("YT", [P, NB])
        is3 = sb("is3", [64, G3])
        place = sb("place", [1, SLOTS], I32)
        source0 = sb("source0", [1, SLOTS], I32)
        dest3 = sb("dest3", [1, SLOTS3], I32)
        expert0 = sb("expert0", [1, NR0], I32)
        expert3 = sb("expert3", [1, G3], I32)
        end0 = sb("end0", [1, E], I32)
        end3 = sb("end3", [1, E], I32)

        xh = [RS[:, 512 * p:512 * p + 256] for p in range(2)]
        xl = [RS[:, 512 * p + 256:512 * p + 512] for p in range(2)]
        hh = [RS[:, 1024 + 1024 * h:1536 + 1024 * h] for h in range(2)]
        hl = [RS[:, 1536 + 1024 * h:2048 + 1024 * h] for h in range(2)]
        xraw = [FS[:, 256 * p:256 * p + 256] for p in range(2)]
        gl = [FS[:, 512 + 512 * h:1024 + 512 * h] for h in range(2)]
        hid = [FS[:, 1536 + 512 * h:2048 + 512 * h] for h in range(2)]
        x1h, x1l, x2h, x2l = ([RS[:, 512 * k + 256 * p:512 * k + 256 * p + 256] for p in range(2)] for k in range(4))
        rh, rl = RS[:, 2048:2176], RS[:, 2176:2304]
        x3h, x3l = RS[:, 0:256], RS[:, 256:512]
        h3h, h3l = RS[:, 512:1024], RS[:, 1024:1536]
        cross = FS[:, 0:256]
        x1 = [FS[:, 256:512], FS[:, 512:768]]
        x2 = [FS[:, 768:1024], FS[:, 1024:1280]]
        mixed = FS[:, 1280:1536]
        ranks = FS[:, 1536:1664]
        gathered = [FS[:, 0:256], FS[:, 256:512]]
        act3, hid3 = FS[:, 512:1024], FS[:, 1024:1536]
        result = [FS[:, 1536:1792], FS[:, 1792:2048]]

        first_raw = [acc[:, NSH + 4 * i:NSH + 4 * (i + 1), :].rearrange("p a d -> p (a d)") for i in range(6)]
        bias_raw = acc[0:64, BIASAT:BIASAT + NBIAS // D, :].rearrange("p a d -> p (a d)")

        rt = routing[0:NB, :]
        iota_slot = rt[:, 0:SLOTS0]
        T1, T2, TW = (rt[:, 136 * k:136 * k + 136] for k in range(1, 4))
        T3 = rt[:, 544:616]
        small = rt[:, 616:900]
        tri, ones = rt[:, 900:964], rt[:, 964:1092]
        condt = rt[:, 1092:1100]
        passed = rt[:, 1100:1100 + 7 * NR0]
        ended = rt[:, 1600:1600 + NR0 + G3]
        maskt = routing[:, 0:DC * D]
        slot_row = routing[0:1, 1100:1100 + SLOTS3]
        tab = [routing[0:1, SLOTS * k:SLOTS * (k + 1)] for k in range(5)]

        bank = [ctx.enter_context(nc.psum_tensor(f"bank{k}", [P, 512], F32)) for k in range(8)]
        gate_ps, up_ps, turn_ps, out_ps = bank[0:2], bank[2:4], bank[4:6], bank[6:8]
        l1_ps, turnx_ps, turn1_ps, low_ps = bank[0:4], bank[4], bank[5], bank[6]
        up3_ps, gate3_ps, turn3_ps, turnh_ps, out3_ps = bank[0], bank[1], bank[2], bank[3], bank[7]

        first_in = [sem(f"first_in{i}") for i in range(6)]
        first_hi, first_ready = sem("first_hi"), sem("first_ready")
        x_in_acc = sem("x_in_acc")
        cond_in, cond_wide_in = sem("cond_in"), sem("cond_wide_in")
        consts_made, bias_room, bias_in = sem("consts_made"), sem("bias_room"), sem("bias_in")
        zeros_made = sem("zeros_made")
        route_step = sem("route_step")
        route_max, route_exp, route_masks = sem("route_max"), sem("route_exp"), sem("route_masks")
        route_counts, route_slots, route_sums = sem("route_counts"), sem("route_slots"), sem("route_sums")
        route_read = sem("route_read")
        tables_ready = sem("tables_ready")
        raw_in = [sem(f"raw_in{k}") for k in range(NRAW)]
        raw_free = sem("raw_free")
        mask_in, masked = sem("mask_in"), sem("masked")
        split_step = sem("split_step")
        rows_step = sem("rows_step")
        b1_in = sem("b1_in")
        xraw_in = [sem(f"xraw_in{p}") for p in range(2)]
        xh_done, xl_done = sem("xh_done"), sem("xl_done")
        gate_done, up_done = sem("gate_done"), sem("up_done")
        gelu_done, hid_done, turn_done = sem("gelu_done"), sem("hid_done"), sem("turn_done")
        hh_done, hl_done = sem("hh_done"), sem("hl_done")
        down_done, acc_done = sem("down_done"), sem("acc_done")
        cross_done, x1_done, t1_done = sem("cross_done"), sem("x1_done"), sem("t1_done")
        x1h_done, x1l_done = sem("x1h_done"), sem("x1l_done")
        l1_done, mix_step, mix_last = sem("l1_done"), sem("mix_step"), sem("mix_last")
        mix_done = sem("mix_done")
        t2_done, x2h_done, x2l_done = sem("t2_done"), sem("x2h_done"), sem("x2l_done")
        low_done, ranks_done = sem("low_done"), sem("ranks_done")
        rh_done, rl_done, l2_done = sem("rh_done"), sem("rl_done"), sem("l2_done")
        x3_done, spread_done = sem("x3_done"), sem("spread_done")
        gathered_done, t3_done = sem("gathered_done"), sem("t3_done")
        x3h_done, x3l_done, pick_done = sem("x3h_done"), sem("x3l_done"), sem("pick_done")
        up3_done, gate3_done = sem("up3_done"), sem("gate3_done")
        silu_done, hid3_done, turnh_done = sem("silu_done"), sem("hid3_done"), sem("turnh_done")
        h3h_done, h3l_done = sem("h3h_done"), sem("h3l_done")
        down3_done = sem("down3_done")
        y_done = sem("y_done")
        out_done = [sem(f"out_done{p}") for p in range(2)]

        block = ctx.enter_context(nc.Block())

        @block.sync
        def _(sp):
            def load_x(g, p, shared=False):
                for j in range(2):
                    if shared:
                        b = 2 * g + j
                    else:
                        b = sp.value_load(source0[0:1, bass.ds(2 * (g - NSH) + j, 1)], min_val=0, max_val=NB - 1)
                    dst = xraw[p].rearrange("p (c j s) -> p c j s", c=DC, j=2)[:, :, j, :]
                    sp.dma_start(dst, xT[bass.ds(b, 1)].rearrange("a p c s -> p (a c) s")).then_inc(xraw_in[p], 16)

            def home_x(pair):
                for j in range(2):
                    src = x.rearrange("(t j) s d -> t j s d", j=2)[bass.ds(2 * pair, 2), j]
                    sp.dma_start(acc[S * j:S * (j + 1), bass.ds(2 * pair, 2), :],
                                 src.rearrange("t s d -> s t d")).then_inc(x_in_acc, 16)

            def first_piece(i):
                sp.dma_start(first_raw[i], w0[0, :, i * PIECE:(i + 1) * PIECE]).then_inc(first_in[i], 16)

            sp.dma_start(condt, cond).then_inc(cond_in, 16)
            first_piece(0)
            load_x(0, 0, shared=True)
            for i in (1, 3, 4, 2, 5):
                first_piece(i)
            load_x(1, 1, shared=True)
            home_x(0)
            sp.wait_ge(xl_done, 1)
            load_x(2, 0, shared=True)
            home_x(1)
            sp.wait_ge(xl_done, 2)
            load_x(3, 1, shared=True)
            for j in range(2):
                sp.dma_start(Y1[S * j:S * (j + 1), :, :],
                             cond.rearrange("(t j) e -> j t e", j=2)[j:j + 1].broadcast_to([S, NSH, E]))\
                    .then_inc(cond_wide_in, 16)
            for e in range(E):
                sp.dma_start(YT[R * e:R * (e + 1), :], condT[e:e + 1, :].broadcast_to([R, NB]))\
                    .then_inc(cond_wide_in, 16)
            sp.dma_start(b1s[:, :], b1.rearrange("(a d) -> a d", a=1).broadcast_to([P, D])).then_inc(b1_in, 16)

            with sp.Fori(2, NSH // 2) as pair:
                for k in range(2):
                    g = 2 * pair + k
                    sp.wait_ge(xl_done, g - 1)
                    load_x(g, k, shared=True)
                    if k == 0:
                        home_x(pair)
            sp.wait_ge(tables_ready, 1)
            with sp.Fori(NSH // 2, G0 // 2) as pair:
                for k in range(2):
                    g = 2 * pair + k
                    sp.wait_ge(xl_done, g - 1)
                    load_x(g, k)

            with sp.Fori(0, G3 // 2) as pair:
                for k in range(2):
                    g = 2 * pair + k
                    sp.wait_ge(y_done, g + 1)
                    for j in range(2):
                        b = sp.value_load(dest3[0:1, bass.ds(2 * g + j, 1)], min_val=0, max_val=NB + SLOTS3 - 1)
                        sp.dma_start(out[bass.ds(b, 1)].rearrange("a s d -> (a s) d"),
                                     result[k][S * j:S * (j + 1), :]).then_inc(out_done[k], 16)
            for k in range(2):
                sp.wait_ge(out_done[k], 32 * (G3 // 2))

        @block.gpsimd
        def _(pool):
            def iota(dst, pattern, base, per_partition):
                return pool.iota(dst, pattern=pattern, base=base, channel_multiplier=per_partition,
                                 allow_small_or_imprecise_dtypes=True)

            iota(iota_slot, [[1, SLOTS0]], 0, 0)
            iota(small[:, 0:E], [[1, E]], -E, 0)
            iota(small[:, 8:9], [[0, 1]], -NONE, 1)
            pool.memset(tri, 1.0)
            pool.memset(one[:, :], 1.0)
            pool.memset(ones, 1.0)
            pool.memset(ident[:, :], 0.0)
            pool.memset(bias_raw, 0.0).then_inc(consts_made, 1)
            pool.wait_ge(consts_made, 1)
            pool.affine_select(out=tri, in_=tri, compare_op=ALU.is_gt, fill=0.0, base=0,
                               pattern=[[1, NB]], channel_multiplier=-1)
            pool.affine_select(out=ident[:, :], in_=ident[:, :], compare_op=ALU.not_equal, fill=1.0,
                               base=0, pattern=[[-1, P]], channel_multiplier=1).then_inc(consts_made, 1)

            def load(k, src):
                pool.dma_start(raw[:, k, :], src).then_inc(raw_in[k], 16)

            def split(k, step, at):
                hi, lo = Wh[:, at:at + PIECE], Wl[:, at:at + PIECE]
                pool.tensor_tensor(hi, raw[:, k, :], one[:, :].broadcast_to([P, PIECE]), ALU.mult).then_inc(split_step, 1)
                pool.wait_ge(split_step, step + 1)
                pool.tensor_tensor(lo, raw[:, k, :], hi.bitcast(F32), ALU.subtract).then_inc(split_step, 1)
                pool.wait_ge(split_step, step + 2)
                pool.sem_inc(raw_free, 1)

            def w0_piece(e, i):
                return w0[bass.ds(e, 1), :, i * PIECE:(i + 1) * PIECE].rearrange("a p n -> p (a n)")

            def expert(e, slot, last=False):
                for i in range(6):
                    k = i % NRAW
                    pool.wait_ge(raw_in[k], 32 * (e - 1) + 16 * (i // NRAW) + 16)
                    split(k, 12 * (e - 1) + 2 * i, slot * EXP0 + i * PIECE)
                    if i < NRAW:
                        load(k, w0_piece(e, i + NRAW))
                    elif not last:
                        load(k, w0_piece(e + 1, i - NRAW))

            def expert_in_ring(e, slot, last=False):
                end = pool.value_load(end0[0:1, bass.ds(e - 3, 1)], min_val=2 * NSH, max_val=2 * G0)
                pool.wait_ge(down_done, end)
                expert(e, slot, last)

            for i in range(NRAW):
                load(i, w0_piece(1, i))
            for q in range(2):
                at = bias_raw[32 * q:32 * q + E, :]
                pool.dma_start(at[:, 0:2 * I3 + D], b3).then_inc(bias_in, 16)
                pool.dma_start(at[0:1, 2 * I3 + D:NBIAS], b2.rearrange("(a d) -> a d", a=1)).then_inc(bias_in, 16)
            expert(1, 1)
            pool.wait_ge(bias_in, 64)
            pool.tensor_tensor(rows3[:, :], bias_raw, one[0:64, :].broadcast_to([64, NBIAS]), ALU.mult)\
                .then_inc(rows_step, 1)
            pool.wait_ge(rows_step, 1)
            lo = rows3[32:64, :]
            pool.tensor_tensor(lo, bias_raw[32:64, :], lo.bitcast(F32), ALU.subtract).then_inc(rows_step, 1)
            pool.wait_ge(rows_step, 2)
            pool.wait_ge(first_ready, 6)
            pool.memset(acc[:, NSH:NB + 1, :], 0.0).then_inc(zeros_made, 1)
            pool.wait_ge(down_done, 2 * NSH)
            expert(2, 0)
            pool.wait_ge(tables_ready, 1)
            with pool.Fori(1, E // 2 - 1) as pair:
                expert_in_ring(2 * pair + 1, 1)
                expert_in_ring(2 * pair + 2, 0)
            expert_in_ring(E - 1, 1)
            expert_in_ring(E, 0, last=True)

            arrived = [32 * E] * NRAW
            srcs = [w1[:, n * PIECE:(n + 1) * PIECE] for n in range(4)] + [w2]
            pool.dma_start(maskt, mask).then_inc(mask_in, 16)
            for n in range(NRAW):
                load(n, srcs[n])
            pool.wait_ge(mask_in, 16)
            end = pool.value_load(end0[0:1, E - 2:E - 1], min_val=2 * NSH, max_val=2 * G0)
            pool.wait_ge(down_done, end)
            for n in range(5):
                k = n % NRAW
                arrived[k] += 16
                pool.wait_ge(raw_in[k], arrived[k])
                if n < 4:
                    m = maskt[:, (n // 2) * D:(n // 2 + 1) * D].unsqueeze(1).broadcast_to([P, 4, D])
                    r4 = raw[:, k, :].rearrange("p (g o) -> p g o", g=4)
                    pool.tensor_tensor(r4, r4, m, ALU.mult).then_inc(masked, 1)
                    pool.wait_ge(masked, n + 1)
                split(k, STEP12 + 2 * n, L1AT + n * PIECE)
                if n + NRAW < 5:
                    load(k, srcs[n + NRAW])

            def w3_piece(e, m):
                return w3[bass.ds(e, 1), :, m * PIECE:(m + 1) * PIECE].rearrange("a p n -> p (a n)")

            def expert3_in(e, slot, last=False):
                for m in range(3):
                    k = (2 + m) % NRAW
                    pool.wait_ge(raw_in[k], arrived[k] + 16 * e + 16)
                    split(k, STEP3 + 6 * e + 2 * m, slot * EXP3 + m * PIECE)
                    if not last:
                        load(k, w3_piece(e + 1, m))

            for m in range(3):
                load((2 + m) % NRAW, w3_piece(0, m))
            pool.wait_ge(down_done, 2 * G0)
            expert3_in(0, 0)
            expert3_in(1, 1)
            pool.wait_ge(l2_done, NSH)
            expert3_in(2, 2)
            expert3_in(3, 3)
            for e in range(4, E):
                end = pool.value_load(end3[0:1, e - 4:e - 3], min_val=1, max_val=G3 + 1)
                pool.wait_ge(down3_done, end)
                expert3_in(e, e % 4, last=(e == E - 1))

        @block.tensor
        def _(pe):
            def route_counts_():
                pe.wait_ge(consts_made, 2)
                pe.wait_ge(route_masks, 1)
                pe.wait_ge(hl_done, 3)
                both = small[:, 64:80]
                pe.matmul(turn_ps[0][0:NB, 0:16], tri, both, start=True, stop=True)
                pe.matmul(turn_ps[0][0:NB, 16:32], ones[:, 0:NB], both, start=True, stop=True).then_inc(route_counts, 1)

            def route_sums_():
                pe.wait_ge(route_slots, 1)
                pe.wait_ge(hl_done, 5)
                colb = small[:, 8:9]
                pe.matmul(turn_ps[0][0:1, 0:SLOTS0], colb, T1, start=True, stop=True)
                pe.matmul(turn_ps[0][0:1, SLOTS0:SLOTS], colb, T3, start=True, stop=True)
                pe.matmul(turn_ps[0][:, SLOTS:SLOTS + SLOTS0], ones, TW, start=True, stop=True).then_inc(route_sums, 1)

            def product(ps, pairs):
                n = len(pairs)
                for i, (ah, al, bh, bl) in enumerate(pairs):
                    pe.matmul(ps, ah, bh, start=(i == 0), stop=False)
                    pe.matmul(ps, ah, bl, start=False, stop=False)
                    mm = pe.matmul(ps, al, bh, start=False, stop=(i == n - 1))
                return mm

            def chunk(t, c):
                return t[:, c * P:(c + 1) * P]

            def weights(at, n):
                return Wh[:, bass.ds(at, n)], Wl[:, bass.ds(at, n)]

            SHARED = -1

            def load_expert(g):
                return pe.value_load(expert0[0:1, bass.ds(g - NSH, 1)], min_val=0, max_val=E - 1)

            def up_gate(g, p, h, e, n2, first=False):
                at = ((e + 1) % 2) * EXP0 + h * HALF0
                if h == 0:
                    pe.wait_ge(xl_done, g + 1)
                if not isinstance(e, int):
                    pe.wait_ge(split_step, 12 * e + 6 * h + 4)
                if not first:
                    pe.wait_ge(hid_done, n2 - 1)
                for ps, k, done in ((gate_ps[h], 0, gate_done), (up_ps[h], 1, up_done)):
                    if first:
                        pe.wait_ge(first_ready, 2 * h + k + 1)
                    product(ps[:, :], [(chunk(xh[p], c), chunk(xl[p], c), *weights(at + k * PIECE + c * 512, 512))
                                       for c in range(DC)]).then_inc(done, 1)

            def turn(h, n2, first=False):
                pe.wait_ge(hid_done, n2 + 1)
                if not first:
                    pe.wait_ge(hl_done, n2 - 1)
                for c in range(4):
                    mm = pe.transpose(chunk(turn_ps[h], c), chunk(hid[h], c), ident[:, :])
                mm.then_inc(turn_done, 1)

            def down(g, p, h, e, n2, first=False):
                at = ((e + 1) % 2) * EXP0 + h * HALF0 + 2 * PIECE
                pe.wait_ge(hl_done, n2 + 1)
                if not isinstance(e, int):
                    pe.wait_ge(split_step, 12 * e + 6 * h + 6)
                elif first:
                    pe.wait_ge(first_ready, 5 + h)
                if h == 0 and not first:
                    pe.wait_ge(acc_done, g - 1)
                ps = out_ps[p][:, 0:D]
                for c in range(4):
                    wh, wl = weights(at + c * D, D)
                    pe.matmul(ps, chunk(hh[h], c), wh, start=(h == 0 and c == 0), stop=False)
                    pe.matmul(ps, chunk(hh[h], c), wl, start=False, stop=False)
                    mm = pe.matmul(ps, chunk(hl[h], c), wh, start=False, stop=(h == 1 and c == 3))
                mm.then_inc(down_done, 1)

            def group(g, p, n=3, e=None, before=None):
                e = load_expert(g) if e is None else e
                up_gate(g, p, 0, e, 2 * g, first=n < 1)
                if n > 0:
                    before = load_expert(g - 1) if before is None else before
                    turn(1, 2 * g - 1, first=n < 2)
                    down(g - 1, 1 - p, 0, before, 2 * g - 2, first=n < 3)
                up_gate(g, p, 1, e, 2 * g + 1, first=n < 1)
                if n == 2 or n == 4:
                    pe.wait_ge(route_read, n // 2)
                turn(0, 2 * g, first=n < 1)
                if n > 0:
                    down(g - 1, 1 - p, 1, before, 2 * g - 1, first=n < 3)

            group(0, 0, n=0, e=SHARED)
            group(1, 1, n=1, e=SHARED, before=SHARED)
            route_counts_()
            group(2, 0, n=2, e=SHARED, before=SHARED)
            route_sums_()
            group(3, 1, n=4, e=SHARED, before=SHARED)
            with pe.Fori(2, NSH // 2) as pair:
                group(2 * pair, 0, e=SHARED, before=SHARED)
                group(2 * pair + 1, 1, e=SHARED, before=SHARED)
            pe.wait_ge(tables_ready, 1)
            group(NSH, 0, before=SHARED)
            group(NSH + 1, 1)
            with pe.Fori(NSH // 2 + 1, G0 // 2) as pair:
                group(2 * pair, 0)
                group(2 * pair + 1, 1)
            last = load_expert(G0 - 1)
            turn(1, 2 * G0 - 1)
            down(G0 - 1, 1, 0, last, 2 * G0 - 2)
            down(G0 - 1, 1, 1, last, 2 * G0 - 1)

            def turn_x(t, ps):
                for c in range(DC):
                    mm = pe.transpose(chunk(ps, c), chunk(t, c), ident[:, :])
                return mm

            def turn_x1(i, p, first=False):
                pe.wait_ge(x1_done, i + 1)
                if first:
                    pe.wait_ge(hl_done, 2 * G0)
                else:
                    pe.wait_ge(x1l_done, i)
                turn_x(x1[p], turn1_ps).then_inc(t1_done, 1)

            def layer1(i, p, k, first=False):
                if k == 0:
                    pe.wait_ge(x1l_done, i + 1)
                if not first:
                    if k < 3:
                        pe.wait_ge(mix_step, 8 * i + 2 * k - 5)
                    else:
                        pe.wait_ge(mix_done, i)
                at = [L1AT + c * E * D + k * 512 for c in range(DC)]
                product(l1_ps[k][:, :], [(chunk(x1h[p], c), chunk(x1l[p], c), Wh[:, at[c]:at[c] + 512],
                                          Wl[:, at[c]:at[c] + 512]) for c in range(DC)]).then_inc(l1_done, 1)

            def low(i, p, first=False):
                pe.wait_ge(x2l_done, i + 1)
                if not first:
                    pe.wait_ge(x3_done, i)
                at = L2AT + 2 * D
                product(low_ps[:, 0:P], [(Wh[:, at + c * P:at + (c + 1) * P], Wl[:, at + c * P:at + (c + 1) * P],
                                          chunk(x2h[p], c), chunk(x2l[p], c)) for c in range(DC)]).then_inc(low_done, 1)

            def layer2(i, p):
                pe.wait_ge(rl_done, i + 1)
                ps = low_ps[:, P:P + D]
                pe.matmul(ps, pick2[:, :], rows3[:, 2 * I3 + D:NBIAS], start=True, stop=False)
                pairs = [(chunk(x2h[p], c), chunk(x2l[p], c), L2AT + c * D) for c in range(DC)] + [(rh, rl, L2AT + 3 * D)]
                for ah, al, at in pairs:
                    pe.matmul(ps, ah, Wh[:, at:at + D], start=False, stop=False)
                    pe.matmul(ps, ah, Wl[:, at:at + D], start=False, stop=False)
                    mm = pe.matmul(ps, al, Wh[:, at:at + D], start=False, stop=(ah is rh))
                mm.then_inc(l2_done, 1)

            def turn_x2(i, p, first=False):
                pe.wait_ge(mix_done, i + 1)
                if not first:
                    pe.wait_ge(x2l_done, i)
                turn_x(x2[p], turnx_ps).then_inc(t2_done, 1)

            pe.sem_inc(down3_done, 1)
            turn_x1(0, 0, first=True)
            pe.wait_ge(split_step, STEP3)
            pe.wait_ge(rows_step, 2)
            pe.wait_ge(acc_done, G0)

            def step(i, p, before=True, after=True, first=False, second=False):
                layer1(i, p, 0, first=first)
                if before:
                    turn_x2(i - 1, 1 - p, first=second)
                layer1(i, p, 1, first=first)
                if before:
                    low(i - 1, 1 - p, first=second)
                if after:
                    turn_x1(i + 1, 1 - p)
                for k in range(2, 4):
                    layer1(i, p, k, first=first)
                if before:
                    layer2(i - 1, 1 - p)

            step(0, 0, before=False, first=True)
            step(1, 1, second=True)
            with pe.Fori(1, NSH // 2 - 1) as pair:
                step(2 * pair, 0)
                step(2 * pair + 1, 1)
            step(NSH - 2, 0)
            step(NSH - 1, 1, after=False)
            turn_x2(NSH - 1, 1)
            low(NSH - 1, 1)
            layer2(NSH - 1, 1)

            def turn_x3(i, p, first=False):
                pe.wait_ge(gathered_done, i + 1)
                if first:
                    pe.wait_ge(mix_done, NSH)
                else:
                    pe.wait_ge(x3l_done, i)
                turn_x(gathered[p], turn3_ps).then_inc(t3_done, 1)

            def load_expert3(i):
                return pe.value_load(expert3[0:1, bass.ds(i, 1)], min_val=0, max_val=E - 1)

            def up_gate3(i, p, e, first=False):
                at = (e % 4) * EXP3
                pe.wait_ge(x3l_done, i + 1)
                pe.wait_ge(split_step, STEP3 + 6 * e + 4)
                if not first:
                    pe.wait_ge(hid3_done, i)
                for ps, k, done in ((up3_ps, 0, up3_done), (gate3_ps, 1, gate3_done)):
                    for c in range(DC):
                        wh, wl = weights(at + k * PIECE + c * 512, 512)
                        pe.matmul(ps[:, :], chunk(x3h, c), wh, start=(c == 0), stop=False)
                        pe.matmul(ps[:, :], chunk(x3h, c), wl, start=False, stop=False)
                        pe.matmul(ps[:, :], chunk(x3l, c), wh, start=False, stop=False)
                    if k == 0:
                        pe.wait_ge(pick_done, i + 1)
                    pe.matmul(ps[:, :], pick3[:, p, :], rows3[:, k * I3:(k + 1) * I3], start=False, stop=True)\
                        .then_inc(done, 1)

            def turn_h(i, first=False):
                pe.wait_ge(hid3_done, i + 1)
                if not first:
                    pe.wait_ge(h3l_done, i)
                for c in range(4):
                    mm = pe.transpose(chunk(turnh_ps, c), chunk(hid3, c), ident[:, :])
                mm.then_inc(turnh_done, 1)

            def down3(i, p, e, first=False):
                at = (e % 4) * EXP3 + 2 * PIECE
                pe.wait_ge(h3l_done, i + 1)
                pe.wait_ge(split_step, STEP3 + 6 * e + 6)
                if not first:
                    pe.wait_ge(y_done, i)
                ps = out3_ps[:, 0:D]
                pe.matmul(ps, pick3[:, p, :], rows3[:, 2 * I3:2 * I3 + D], start=True, stop=False)
                for c in range(4):
                    wh, wl = weights(at + c * D, D)
                    pe.matmul(ps, chunk(h3h, c), wh, start=False, stop=False)
                    pe.matmul(ps, chunk(h3h, c), wl, start=False, stop=False)
                    mm = pe.matmul(ps, chunk(h3l, c), wh, start=False, stop=(c == 3))
                mm.then_inc(down3_done, 1)

            def step3(i, p, before=True, after=True, after2=True, first=False, second=False):
                if before:
                    e_before = load_expert3(i - 1)
                if after:
                    e_after = load_expert3(i + 1)
                if before:
                    down3(i - 1, 1 - p, e_before, first=second)
                turn_h(i, first=first)
                if after:
                    up_gate3(i + 1, 1 - p, e_after)
                if after2:
                    turn_x3(i + 2, p)

            turn_x3(0, 0, first=True)
            up_gate3(0, 0, load_expert3(0), first=True)
            turn_x3(1, 1)
            step3(0, 0, before=False, first=True)
            step3(1, 1, second=True)
            with pe.Fori(1, G3 // 2 - 1) as pair:
                step3(2 * pair, 0)
                step3(2 * pair + 1, 1)
            step3(G3 - 2, 0, after2=False)
            step3(G3 - 1, 1, after=False, after2=False)
            down3(G3 - 1, 1, load_expert3(G3 - 1))

        @block.scalar
        def _(act):
            act.wait_ge(route_max, 1)
            act.activation(small[:, 32:40], condt, ACT.Exp, bias=small[:, 17:18],
                           accum_out=small[:, 18:19]).then_inc(route_exp, 1)

            def split_x(g, p, first=False):
                act.wait_ge(xraw_in[p], 16 * (g - p) + 32)
                if not first:
                    act.wait_ge(up_done, 2 * g - 2)
                act.activation(xh[p], xraw[p], ACT.Copy).then_inc(xh_done, 1)

            def gelu(h, n2, first=False):
                act.wait_ge(gate_done, n2 + 1)
                if not first:
                    act.wait_ge(hid_done, n2 - 1)
                act.activation(gl[h], gate_ps[h][:, :], ACT.Gelu_apprx_tanh).then_inc(gelu_done, 1)

            def hidden_hi(h, n2, first=False):
                act.wait_ge(turn_done, n2 + 1)
                if not first:
                    act.wait_ge(down_done, n2 - 1)
                act.activation(hh[h], turn_ps[h][:, :], ACT.Copy).then_inc(hh_done, 1)

            def group(g, p, n=3, after=True):
                gelu(0, 2 * g, first=n < 1)
                if n > 0:
                    hidden_hi(1, 2 * g - 1, first=n < 2)
                if after:
                    split_x(g + 1, 1 - p, first=n < 1)
                gelu(1, 2 * g + 1, first=n < 1)
                hidden_hi(0, 2 * g, first=n < 1)

            def first_piece(i):
                act.wait_ge(first_in[i], 16)
                act.activation(Wh[:, i * PIECE:(i + 1) * PIECE], first_raw[i], ACT.Copy).then_inc(first_hi, 1)

            first_piece(0)
            split_x(0, 0, first=True)
            for i in (1, 3, 4, 2, 5):
                first_piece(i)
            group(0, 0, n=0)
            group(1, 1, n=1)
            with act.Fori(1, G0 // 2 - 1) as pair:
                group(2 * pair, 0)
                group(2 * pair + 1, 1)
            group(G0 - 2, 0)
            group(G0 - 1, 1, after=False)
            hidden_hi(1, 2 * G0 - 1)

            def hi(arrived, count, dst, src, done, free=None, freed=None):
                act.wait_ge(arrived, count)
                if free is not None:
                    act.wait_ge(free, freed)
                act.activation(dst, src, ACT.Copy).then_inc(done, 1)

            def at_place(t, half, b):
                return t[half, bass.ds(b, 1), :].rearrange("p a d -> p (a d)")

            halves = (slice(0, S), slice(S, P))

            def cross_over(i, first=False):
                if not first:
                    act.wait_ge(x1_done, i)
                for j in range(2):
                    op = act.activation(cross[halves[j], :], at_place(acc, halves[1 - j], NSH + i), ACT.Copy)
                op.then_inc(cross_done, 1)

            def spread(i):
                act.wait_ge(x3_done, i + 1)
                for j in range(2):
                    op = act.activation(at_place(acc, halves[1 - j], NSH + i), at_place(acc, halves[j], i), ACT.Copy)
                op.then_inc(spread_done, 1)

            def step(i, p, before=True, after=True, after2=True, first=False, second=False, third=False):
                if before:
                    hi(t2_done, i, x2h[1 - p], turnx_ps[:, 0:D], x2h_done,
                       *((None, None) if second or third else (l2_done, i - 2)))
                if after2:
                    cross_over(i + 2)
                if before:
                    hi(ranks_done, i, rh, ranks, rh_done, *((None, None) if second else (l2_done, i - 1)))
                if after:
                    hi(t1_done, i + 2, x1h[1 - p], turn1_ps[:, 0:D], x1h_done,
                       *((None, None) if first else (l1_done, 4 * i)))
                if before and not second:
                    spread(i - 2)

            act.wait_ge(acc_done, G0)
            cross_over(0, first=True)
            cross_over(1)
            hi(t1_done, 1, x1h[0], turn1_ps[:, 0:D], x1h_done)
            step(0, 0, before=False, first=True)
            step(1, 1, second=True)
            step(2, 0, third=True)
            step(3, 1)
            with act.Fori(2, NSH // 2 - 1) as pair:
                step(2 * pair, 0)
                step(2 * pair + 1, 1)
            step(NSH - 2, 0, after2=False)
            step(NSH - 1, 1, after=False, after2=False)
            hi(t2_done, NSH, x2h[1], turnx_ps[:, 0:D], x2h_done, l2_done, NSH - 2)
            hi(ranks_done, NSH, rh, ranks, rh_done, l2_done, NSH - 1)
            spread(NSH - 2)
            spread(NSH - 1)
            act.wait_ge(spread_done, NSH)

            def gather(i, p, first=False):
                if not first:
                    act.wait_ge(t3_done, i - 1)
                for j in range(2):
                    b = act.value_load(place[0:1, bass.ds(SLOTS0 + 2 * i + j, 1)], min_val=0, max_val=NONE)
                    op = act.activation(gathered[p][halves[j], :], at_place(acc, halves[j], b), ACT.Copy)
                op.then_inc(gathered_done, 1)

            def pick(i, p, first=False):
                if not first:
                    act.wait_ge(down3_done, i)
                act.activation(pick3[:, p, :], is3[:, bass.ds(i, 1)].broadcast_to([64, P]), ACT.Copy)\
                    .then_inc(pick_done, 1)

            def silu(i, first=False):
                act.wait_ge(up3_done, i + 1)
                if not first:
                    act.wait_ge(hid3_done, i)
                act.activation(act3, up3_ps[:, :], ACT.Silu).then_inc(silu_done, 1)

            def step3(i, p, before=True, after=True, after2=True, first=False, second=False):
                if before:
                    hi(turnh_done, i, h3h, turnh_ps[:, :], h3h_done,
                       *((None, None) if second else (down3_done, i)))
                if after2:
                    gather(i + 2, p)
                silu(i, first=first)
                if after:
                    hi(t3_done, i + 2, x3h, turn3_ps[:, 0:D], x3h_done, gate3_done, i + 1)
                    pick(i + 1, 1 - p, first=first)

            for i in range(2):
                gather(i, i, first=True)
            hi(t3_done, 1, x3h, turn3_ps[:, 0:D], x3h_done)
            pick(0, 0, first=True)
            step3(0, 0, before=False, first=True)
            step3(1, 1, second=True)
            with act.Fori(1, G3 // 2 - 1) as pair:
                step3(2 * pair, 0)
                step3(2 * pair + 1, 1)
            step3(G3 - 2, 0, after2=False)
            step3(G3 - 1, 1, after=False, after2=False)
            hi(turnh_done, G3, h3h, turnh_ps[:, :], h3h_done, down3_done, G3)

        @block.vector
        def _(dve):
            count = [0]

            def done(op):
                count[0] += 1
                op.then_inc(route_step, 1)
                dve.wait_ge(route_step, count[0])

            TT, TS, STT = dve.tensor_tensor, dve.tensor_scalar, dve.scalar_tensor_tensor
            eid = small[:, 0:E]
            colb = small[:, 8:9]
            def col(k):
                return small[:, k:k + 1]
            m1, i1, m2, i2, nm1, ssum, w1c, w2c, rc, pos1, pos2, pos3 = (
                col(k) for k in (16, 19, 20, 21, 17, 18, 22, 23, 24, 25, 26, 27))
            ex, junk = small[:, 32:40], small[:, 40:48]
            M1, M2 = small[:, 48:56], small[:, 56:64]
            both = small[:, 64:80].rearrange("b (a e) -> b a e", a=2)
            Mt, M3 = both[:, 0, :], both[:, 1, :]
            cond2 = small[:, 80:88]

            def first_of(values, top, index, mask):
                done(TS(junk, values, top, None, ALU.is_ge))
                done(TT(junk, junk, eid, ALU.mult))
                done(dve.tensor_reduce(index, junk, AX.X, ALU.min))
                done(TS(mask, eid, index, None, ALU.is_equal))

            def route_choose():
                dve.wait_ge(cond_in, 16)
                done(dve.tensor_reduce(m1, condt, AX.X, ALU.max))
                TS(nm1, m1, -1.0, None, ALU.mult).then_inc(route_max, 1)
                dve.wait_ge(consts_made, 2)
                first_of(condt, m1, i1, M1)
                done(STT(cond2, M1, -3.0e38, condt, ALU.mult, ALU.add))
                done(dve.tensor_reduce(m2, cond2, AX.X, ALU.max))
                first_of(cond2, m2, i2, M2)
                TT(Mt, M1, M2, ALU.add)
                dve.tensor_copy(M3, M1).then_inc(route_masks, 1)

            def blocks(k):
                return small[:, k:k + 16].rearrange("b (a e) -> b a e", a=2)

            def route_weights():
                dve.wait_ge(route_exp, 1)
                done(dve.reciprocal(rc, ssum))
                done(TS(ex, ex, rc, None, ALU.mult))
                for m, w in ((M1, w1c), (M2, w2c)):
                    done(TT(junk, ex, m, ALU.mult))
                    done(dve.tensor_reduce(w, junk, AX.X, ALU.add))
                done(TT(rc, w1c, w2c, ALU.add))
                done(dve.reciprocal(rc, rc))
                for w in (w1c, w2c):
                    done(TT(w, w, rc, ALU.mult))
                    done(TS(col(28), w, TOP_SCALE, None, ALU.mult))
                    done(STT(w, w, 1.0 - TOP_SCALE, col(28), ALU.mult, ALU.add))

            groups, sum1, sum2, ends, begins, places = (blocks(k) for k in (104, 120, 136, 152, 168, 184))
            counts = small[:, 200:232]

            def route_places():
                ints = small[:, 88:104].bitcast(I32)
                dve.wait_ge(route_counts, 1)
                dve.tensor_copy(counts, turn_ps[0][0:NB, 0:32]).then_inc(route_read, 1)
                dve.wait_ge(route_read, 1)
                done(TS(ints, counts[:, 16:32], 1.0, None, ALU.add))
                done(TS(ints, ints, 1, None, ALU.logical_shift_right))
                done(dve.tensor_copy(groups, ints.rearrange("b (a e) -> b a e", a=2)))
                for a, b, k in ((groups, sum1, 1), (sum1, sum2, 2), (sum2, ends, 4)):
                    dve.tensor_copy(b[:, :, 0:k], a[:, :, 0:k])
                    done(TT(b[:, :, k:E], a[:, :, k:E], a[:, :, 0:E - k], ALU.add))
                done(TT(begins, ends, groups, ALU.subtract))
                done(STT(places, begins, 2.0, counts[:, 0:16].rearrange("b (a e) -> b a e", a=2), ALU.mult, ALU.add))
                for m, a, pos in ((M1, 0, pos1), (M2, 0, pos2), (M1, 1, pos3)):
                    done(TT(junk, places[:, a, :], m, ALU.mult))
                    done(dve.tensor_reduce(pos, junk, AX.X, ALU.add))
                TS(T1, iota_slot, pos1, None, ALU.is_equal)
                TS(T3, iota_slot[:, 0:SLOTS3], pos3, None, ALU.is_equal)
                done(TS(T2, iota_slot, pos2, None, ALU.is_equal))
                done(TS(TW, T1, w1c, None, ALU.mult))
                done(STT(TW, T2, w2c, TW, ALU.mult, ALU.add))
                TT(T1, T1, T2, ALU.add).then_inc(route_slots, 1)

            def route_experts():
                for a, g, n in ((0, 0, NR0), (1, NR0, G3)):
                    v = passed[:, 0:n * (E - 1)].rearrange("b (n k) -> b n k", n=n)
                    done(TT(v, iota_slot[:, 0:n].unsqueeze(2).broadcast_to([NB, n, E - 1]),
                            ends[:, a, 0:E - 1].unsqueeze(1).broadcast_to([NB, n, E - 1]), ALU.is_ge))
                    done(dve.tensor_reduce(ended[:, g:g + n], v, AX.X, ALU.add))
                dve.tensor_copy(expert0[:, :], ended[0:1, 0:NR0])
                dve.tensor_copy(expert3[:, :], ended[0:1, NR0:])
                TS(end0[:, :], ends[0:1, 0, :], float(NSH), 2.0, ALU.add, ALU.mult)
                TS(end3[:, :], ends[0:1, 1, :], 1.0, None, ALU.add)
                row, row32 = col(9), col(10)
                done(TS(row, colb, float(NONE), None, ALU.add))
                done(TS(row32, row, 32.0, -32.0, ALU.is_ge, ALU.mult))
                done(TT(row32, row, row32, ALU.add))
                TS(is3[:, :], ended[:, NR0:], row32, None, ALU.is_equal)
                done(TS(pick2[:, :], row32.broadcast_to([64, P]), 0.0, None, ALU.is_equal))

            def route_tables():
                dve.wait_ge(route_sums, 1)
                done(dve.tensor_copy(slot_row, iota_slot[0:1, 0:SLOTS3]))
                batch, flag, part = (tab[k] for k in range(3))
                whole, odd = (tab[k].bitcast(I32) for k in (3, 4))
                for j in range(2):
                    half = slice(S * j, S * (j + 1))
                    dve.tensor_copy(weight0[half, :], turn_ps[0][half, SLOTS + j:SLOTS + SLOTS0:2])
                TS(batch, turn_ps[0][0:1, 0:SLOTS], float(NONE), None, ALU.add).then_inc(route_read, 1)
                dve.wait_ge(route_read, 2)
                TS(source0[:, :], batch, float(NB - 1), None, ALU.min)
                done(dve.tensor_copy(whole, batch))
                done(TS(odd, whole, 1, None, ALU.bitwise_and))
                done(TS(whole, whole, 1, None, ALU.logical_shift_right))
                for j in range(2):
                    op = TS(flag[:, j::2], odd[:, j::2], float(j), float(NSH), ALU.not_equal, ALU.mult)
                done(op)
                done(TT(part, whole, flag, ALU.add))
                done(TS(flag, batch, float(NONE), float(NB), ALU.is_ge, ALU.mult))
                done(TT(part, part, flag, ALU.add))
                TS(place[:, :], part, float(NONE), None, ALU.min)
                b3_, f3 = batch[:, SLOTS0:SLOTS], flag[:, SLOTS0:SLOTS]
                done(TS(f3, f3, 1.0 / NB, None, ALU.mult))
                done(TT(f3, f3, slot_row[:, :], ALU.mult))
                done(TT(dest3[:, :], b3_, f3, ALU.add))
                TS(YT[:, :], YT[:, :], 2.0, None, ALU.mult).then_inc(tables_ready, 1)

            def split_x(g, p):
                dve.wait_ge(xh_done, g + 1)
                TT(xl[p], xraw[p], xh[p].bitcast(F32), ALU.subtract).then_inc(xl_done, 1)

            def hidden(h, n2, first=False):
                dve.wait_ge(gelu_done, n2 + 1)
                dve.wait_ge(up_done, n2 + 1)
                if not first:
                    dve.wait_ge(turn_done, n2 - 1)
                TT(hid[h], up_ps[h][:, :], gl[h], ALU.mult).then_inc(hid_done, 1)

            def hidden_lo(h, n2):
                dve.wait_ge(hh_done, n2 + 1)
                TT(hl[h], turn_ps[h][:, :], hh[h].bitcast(F32), ALU.subtract).then_inc(hl_done, 1)

            def add_shared(g, p):
                dve.wait_ge(down_done, 2 * g + 2)
                dve.wait_ge(x_in_acc, 16 * (g - p) + 32)
                at = acc[:, bass.ds(g, 1), :].rearrange("p a d -> p (a d)")
                TT(at, out_ps[p][:, 0:D], at, ALU.add).then_inc(acc_done, 1)

            def add(g, p):
                dve.wait_ge(down_done, 2 * g + 2)
                dve.wait_ge(acc_done, g)
                for j in range(2):
                    b = dve.value_load(place[0:1, bass.ds(2 * (g - NSH) + j, 1)], min_val=0, max_val=NONE)
                    half = slice(S * j, S * (j + 1))
                    at = acc[half, bass.ds(b, 1), :].rearrange("p a d -> p (a d)")
                    op = STT(at, out_ps[p][half, 0:D], weight0[half, bass.ds(g - NSH, 1)], at, ALU.mult, ALU.add)
                op.then_inc(acc_done, 1)

            def group(g, p, n=3, after=True, add_before=add):
                hidden(0, 2 * g, first=n < 1)
                if n > 0:
                    hidden_lo(1, 2 * g - 1)
                if after:
                    split_x(g + 1, 1 - p)
                hidden(1, 2 * g + 1, first=n < 1)
                hidden_lo(0, 2 * g)
                if n > 0:
                    add_before(g - 1, 1 - p)

            def first_piece(n, i):
                dve.wait_ge(first_hi, n)
                TT(Wl[:, i * PIECE:(i + 1) * PIECE], first_raw[i], Wh[:, i * PIECE:(i + 1) * PIECE].bitcast(F32),
                   ALU.subtract).then_inc(first_ready, 1)

            route_choose()
            first_piece(1, 0)
            split_x(0, 0)
            for n, i in enumerate((1, 3, 4, 2, 5)):
                first_piece(n + 2, i)
            group(0, 0, n=0)
            group(1, 1, n=1, add_before=add_shared)
            route_weights()
            route_places()
            group(2, 0, add_before=add_shared)
            route_experts()
            dve.wait_ge(cond_wide_in, 160)
            route_tables()
            group(3, 1, add_before=add_shared)
            with dve.Fori(2, NSH // 2) as pair:
                group(2 * pair, 0, add_before=add_shared)
                group(2 * pair + 1, 1, add_before=add_shared)
            group(NSH, 0, add_before=add_shared)
            dve.wait_ge(zeros_made, 1)
            group(NSH + 1, 1)
            with dve.Fori(NSH // 2 + 1, G0 // 2 - 1) as pair:
                group(2 * pair, 0)
                group(2 * pair + 1, 1)
            group(G0 - 2, 0)
            group(G0 - 1, 1, after=False)
            hidden_lo(1, 2 * G0 - 1)
            add(G0 - 1, 1)

            def home(i):
                return acc[:, bass.ds(i, 1), :].rearrange("p a d -> p (a d)")

            def join(i, p, first=False):
                dve.wait_ge(cross_done, i + 1)
                if first:
                    dve.wait_ge(acc_done, G0)
                else:
                    dve.wait_ge(t1_done, i - 1)
                TT(x1[p], cross, home(i), ALU.add).then_inc(x1_done, 1)

            def mix_start(i, p, first=False):
                if not first:
                    dve.wait_ge(t2_done, i - 1)
                    dve.wait_ge(x3_done, i - 1)
                TT(x2[p], x1[p], b1s[:, :], ALU.add).then_inc(mix_step, 1)

            def mix(i, p, k):
                for q in range(2):
                    y = Y1[:, bass.ds(i, 1), 2 * k + q]
                    ps = l1_ps[k][:, q * D:(q + 1) * D]
                    if k == 0 and q == 0:
                        dve.wait_ge(l1_done, 4 * i + 1)
                        dve.wait_ge(mix_step, 8 * i + 1)
                    if k == 0 and q == 1:
                        TS(mixed, ps, y, None, ALU.mult).then_inc(mix_step, 1)
                        return
                    if q == 0:
                        dve.wait_ge(l1_done, 4 * i + k + 1)
                    if k < 3:
                        sum_ = (x2[p], mixed)[q]
                        if k > 0:
                            dve.wait_ge(mix_step, 8 * i + 2 * k + q)
                        STT(sum_, ps, y, sum_, ALU.mult, ALU.add).then_inc(mix_step, 1)
                    else:
                        if q == 0:
                            dve.wait_ge(mix_step, 8 * i + 8)
                        else:
                            dve.wait_ge(mix_last, i + 1)
                        STT(x2[p], ps, y, x2[p], ALU.mult, ALU.add).then_inc(mix_last if q == 0 else mix_done, 1)

            def mix_sums(i, p):
                dve.wait_ge(mix_step, 8 * i + 7)
                TT(x2[p], x2[p], mixed, ALU.add).then_inc(mix_step, 1)

            def lo(i, dst, src, hi, hi_done, done_):
                dve.wait_ge(hi_done, i)
                TT(dst, src, hi.bitcast(F32), ALU.subtract).then_inc(done_, 1)

            def weigh(i):
                dve.wait_ge(low_done, i + 1)
                for j in range(2):
                    op = TS(ranks[:, S * j:S * (j + 1)], low_ps[:, S * j:S * (j + 1)],
                            YT[:, bass.ds(2 * i + j, 1)], None, ALU.mult)
                op.then_inc(ranks_done, 1)

            def finish2(i, p):
                dve.wait_ge(l2_done, i + 1)
                dve.wait_ge(mix_done, i + 1)
                TT(home(i), low_ps[:, P:P + D], x2[p], ALU.add).then_inc(x3_done, 1)

            def step(i, p, before=True, after=True, after2=True, first=False, second=False):
                if before and not second:
                    finish2(i - 2, p)
                mix_start(i, p, first=first or second)
                if before:
                    lo(i, x2l[1 - p], turnx_ps[:, 0:D], x2h[1 - p], x2h_done, x2l_done)
                mix(i, p, 0)
                mix(i, p, 1)
                if before:
                    weigh(i - 1)
                    dve.wait_ge(ranks_done, i)
                    lo(i, rl, ranks, rh, rh_done, rl_done)
                if after:
                    lo(i + 2, x1l[1 - p], turn1_ps[:, 0:D], x1h[1 - p], x1h_done, x1l_done)
                if after2:
                    join(i + 2, p)
                mix(i, p, 2)
                mix_sums(i, p)
                mix(i, p, 3)

            dve.wait_ge(b1_in, 16)
            join(0, 0, first=True)
            join(1, 1, first=True)
            lo(1, x1l[0], turn1_ps[:, 0:D], x1h[0], x1h_done, x1l_done)
            step(0, 0, before=False, first=True)
            step(1, 1, second=True)
            with dve.Fori(1, NSH // 2 - 1) as pair:
                step(2 * pair, 0)
                step(2 * pair + 1, 1)
            step(NSH - 2, 0, after2=False)
            step(NSH - 1, 1, after=False, after2=False)
            finish2(NSH - 2, 0)
            lo(NSH, x2l[1], turnx_ps[:, 0:D], x2h[1], x2h_done, x2l_done)
            weigh(NSH - 1)
            dve.wait_ge(ranks_done, NSH)
            lo(NSH, rl, ranks, rh, rh_done, rl_done)
            finish2(NSH - 1, 1)

            def hidden3(i, first=False):
                dve.wait_ge(silu_done, i + 1)
                dve.wait_ge(gate3_done, i + 1)
                if not first:
                    dve.wait_ge(turnh_done, i)
                TT(hid3, gate3_ps[:, :], act3, ALU.mult).then_inc(hid3_done, 1)

            def finish3(i, p, first=False):
                dve.wait_ge(down3_done, i + 2)
                if not first:
                    dve.wait_ge(out_done[p], 16 * (i - p))
                for j in range(2):
                    b = dve.value_load(place[0:1, bass.ds(SLOTS0 + 2 * i + j, 1)], min_val=0, max_val=NONE)
                    half = slice(S * j, S * (j + 1))
                    op = TT(result[p][half, :], out3_ps[half, 0:D],
                            acc[half, bass.ds(b, 1), :].rearrange("p a d -> p (a d)"), ALU.add)
                op.then_inc(y_done, 1)

            def step3(i, p, before=True, after=True, first=False, early=False):
                if before:
                    lo(i, h3l, turnh_ps[:, :], h3h, h3h_done, h3l_done)
                hidden3(i, first=first)
                if after:
                    lo(i + 2, x3l, turn3_ps[:, 0:D], x3h, x3h_done, x3l_done)
                if before:
                    finish3(i - 1, 1 - p, first=early)

            dve.wait_ge(spread_done, NSH)
            lo(1, x3l, turn3_ps[:, 0:D], x3h, x3h_done, x3l_done)
            step3(0, 0, before=False, first=True)
            step3(1, 1, early=True)
            step3(2, 0, early=True)
            step3(3, 1)
            with dve.Fori(2, G3 // 2 - 1) as pair:
                step3(2 * pair, 0)
                step3(2 * pair + 1, 1)
            step3(G3 - 2, 0)
            step3(G3 - 1, 1, after=False)
            lo(G3, h3l, turnh_ps[:, :], h3h, h3h_done, h3l_done)
            finish3(G3 - 1, 1)


def kernel(x, cond_8, L0_cond_skill_gate, L0_cond_skill_up, L0_cond_skill_down, L0_cond_shared_gate,
           L0_cond_shared_up, L0_cond_shared_down, L1_cond_weight, L1_cond_mask, L1_cond_bias,
           L2_cond_W_base, L2_cond_b_base, L2_cond_As, L2_cond_Bs, L3_cond_W_up, L3_cond_b_up,
           L3_cond_W_gate, L3_cond_b_gate, L3_cond_W_down, L3_cond_b_down):
    import numpy as np

    import concourse.bacc as bacc
    from concourse.bass_utils import run_bass_kernel_spmd

    def rows(w):
        w = np.asarray(w)
        return np.swapaxes(w.reshape(*w.shape[:-2], w.shape[-2] // P, P, w.shape[-1]), -3, -2)

    x = np.asarray(x)
    gate = rows(np.concatenate([np.asarray(L0_cond_shared_gate)[None], np.asarray(L0_cond_skill_gate)]))
    up = rows(np.concatenate([np.asarray(L0_cond_shared_up)[None], np.asarray(L0_cond_skill_up)]))
    down = rows(np.concatenate([np.asarray(L0_cond_shared_down)[None], np.asarray(L0_cond_skill_down)]))
    parts = []
    for h in range(2):
        parts += [gate[..., 512 * h:512 * (h + 1)].reshape(E + 1, P, PIECE),
                  up[..., 512 * h:512 * (h + 1)].reshape(E + 1, P, PIECE),
                  down[:, :, 4 * h:4 * (h + 1)].reshape(E + 1, P, PIECE)]
    w1 = np.swapaxes(rows(np.swapaxes(np.asarray(L1_cond_weight), 1, 2)), 0, 1)
    w1 = np.swapaxes(w1, 1, 2).reshape(P, DC * E * D)
    mask = rows(np.asarray(L1_cond_mask).T).reshape(P, DC * D)
    w2 = np.concatenate([rows(np.asarray(L2_cond_W_base).T).reshape(P, DC * D),
                         rows(np.asarray(L2_cond_As).reshape(E * R, D).T).reshape(P, DC * E * R),
                         np.swapaxes(np.asarray(L2_cond_Bs), 1, 2).reshape(E * R, D)], axis=1)
    w3 = np.concatenate([rows(np.swapaxes(np.asarray(w), 1, 2)).reshape(E, P, PIECE)
                         for w in (L3_cond_W_up, L3_cond_W_gate, L3_cond_W_down)], axis=2)
    b3 = np.concatenate([np.asarray(b) for b in (L3_cond_b_up, L3_cond_b_gate, L3_cond_b_down)], axis=1)
    ins = {
        "x": x,
        "xT": rows(np.swapaxes(x, 1, 2)),
        "cond": np.asarray(cond_8), "condT": np.asarray(cond_8).T,
        "w0": np.concatenate(parts, axis=2),
        "w1": w1, "mask": mask, "b1": np.asarray(L1_cond_bias),
        "w2": w2, "b2": np.asarray(L2_cond_b_base),
        "w3": w3, "b3": b3,
    }
    ins = {k: np.ascontiguousarray(v) for k, v in ins.items()}
    nc = bacc.Bacc("TRN2", target_bir_lowering=False, num_devices=1, dynamic_dma_scratch_size=DMA_RING)
    aps = {k: nc.dram_tensor(f"in_{k}", v.shape, mybir.dt.from_np(v.dtype), kind="ExternalInput").ap()
           for k, v in ins.items()}
    out = nc.dram_tensor("out_rows", (NB + SLOTS3, S, D), F32, kind="ExternalOutput").ap()
    build(nc, **aps, out=out)
    result = run_bass_kernel_spmd(nc, [{f"in_{k}": v for k, v in ins.items()}], core_ids=[0])
    return result.results[0]["out_rows"][:NB]
```

```python
from contextlib import ExitStack

import concourse.bass as bass
from concourse import mybir

F32 = mybir.dt.float32
F32R = mybir.dt.float32r
I32 = mybir.dt.int32
ALU = mybir.AluOpType
ACT = mybir.ActivationFunctionType
AX = mybir.AxisListType

P = 128
NB, S, D = 64, 64, 256
E = 8
DC = D // P
I0, I3 = 1024, 512
R, ALPHA = 16, 32.0
NSH = NB // 2
NR0 = (2 * NB + E) // 2
FIRST = 4
TURNLESS = 2 * (NSH - FIRST)
G0 = NSH + NR0
G3 = (NB + E) // 2
SLOTS0, SLOTS3 = 2 * NR0, 2 * G3
SLOTS = SLOTS0 + SLOTS3
PIECE = 1024
NRAW = 3
HALF0 = 3 * PIECE
EXP0 = 2 * HALF0
EXP3 = 3 * PIECE
L1AT = EXP0
L2AT = L1AT + DC * E * D
NBIAS = 2 * I3 + D
BIASAT = NSH + EXP0 // D
NONE = NB
TOP_SCALE = 1.0 / 12
WARM_UP = 12
DMA_RING = 6144
STEP12 = 12 * E
STEP3 = STEP12 + 10


def build(nc, x, xT, cond, w0, w1, mask, b1, w2, b2, w3, b3, out):
    with ExitStack() as ctx:
        def sb(name, shape, dt=F32):
            return ctx.enter_context(nc.sbuf_tensor(name, shape, dt))

        def sem(name):
            return ctx.enter_context(nc.semaphore(name))

        acc = sb("acc", [P, NB + 1, D])
        Wh = sb("Wh", [P, 2 * EXP0], F32R)
        Wl = sb("Wl", [P, 2 * EXP0], F32R)
        raw = sb("raw", [P, NRAW, PIECE])
        RS = sb("RS", [P, 4096], F32R)
        FS = sb("FS", [P, 2560])
        routing = sb("routing", [P, 1720])
        rows3 = sb("rows3", [64, NBIAS], F32R)
        pick3 = sb("pick3", [64, 2, P], F32R)
        ident = sb("ident", [P, P])
        one = sb("one", [P, 1])
        weight0 = sb("weight0", [P, NR0])
        Y1 = sb("Y1", [P, NSH, E])
        is3 = sb("is3", [64, G3])
        place = sb("place", [1, SLOTS], I32)
        source0 = sb("source0", [1, SLOTS0], I32)
        dest3 = sb("dest3", [1, SLOTS3], I32)
        turn0 = sb("turn0", [1, NR0], I32)
        turn3 = sb("turn3", [1, G3], I32)
        chosen0 = sb("chosen0", [1, E], I32)
        chosen3 = sb("chosen3", [1, E], I32)
        end0 = sb("end0", [1, E], I32)
        end3 = sb("end3", [1, E], I32)

        XSET = [RS[:, at:at + 1024] for at in (0, 3072)]
        xh = [[xs[:, 512 * p:512 * p + 256] for p in range(2)] for xs in XSET]
        xl = [[xs[:, 512 * p + 256:512 * p + 512] for p in range(2)] for xs in XSET]
        hh = [RS[:, 1024 + 1024 * h:1536 + 1024 * h] for h in range(2)]
        hl = [RS[:, 1536 + 1024 * h:2048 + 1024 * h] for h in range(2)]
        xraw = [FS[:, 256 * p:256 * p + 256] for p in range(2)]
        gl = [FS[:, 512 + 512 * h:1024 + 512 * h] for h in range(2)]
        hid = [FS[:, 1536 + 512 * h:2048 + 512 * h] for h in range(2)]
        x1h, x1l, x2h, x2l = ([RS[:, 512 * k + 256 * p:512 * k + 256 * p + 256] for p in range(2)] for k in range(4))
        rh, rl = RS[:, 2048:2176], RS[:, 2176:2304]
        x3h, x3l = RS[:, 0:256], RS[:, 256:512]
        h3h, h3l = RS[:, 512:1024], RS[:, 1024:1536]
        cross = FS[:, 0:256]
        x1 = [FS[:, 256:512], FS[:, 512:768]]
        x2 = [FS[:, 768:1024], FS[:, 1024:1280]]
        mixed = FS[:, 1280:1536]
        ranks = FS[:, 1536:1664]
        gathered = [FS[:, 0:256], FS[:, 256:512]]
        act3, hid3 = FS[:, 512:1024], FS[:, 1024:1536]
        result = [FS[:, 1536:1792], FS[:, 1792:2048]]

        first_raw = [acc[:, NSH + 4 * i:NSH + 4 * (i + 1), :].rearrange("p a d -> p (a d)") for i in range(6)]
        bias_raw = acc[0:64, BIASAT:BIASAT + NBIAS // D, :].rearrange("p a d -> p (a d)")

        rt = routing[0:NB, :]
        iota_slot = rt[:, 0:SLOTS0]
        T1, T2, TW = (rt[:, 136 * k:136 * k + 136] for k in range(1, 4))
        T3 = rt[:, 544:616]
        small = rt[:, 616:900]
        tri, ones = rt[:, 900:964], rt[:, 964:1092]
        condt = rt[:, 1092:1100]
        passed = rt[:, 1100:1100 + 7 * NR0]
        ended = rt[:, 1600:1600 + NR0]
        expert_of = rt[:, 1600 + NR0:1600 + NR0 + G3]
        maskt = routing[:, 0:DC * D]
        b1s, b2s = (routing[:, k * D:(k + 1) * D] for k in (DC, DC + 1))
        slot_row = routing[0:1, 1100:1100 + SLOTS3]
        tab = [routing[0:1, SLOTS * k:SLOTS * (k + 1)] for k in range(5)]

        bank = [ctx.enter_context(nc.psum_tensor(f"bank{k}", [P, 512], F32)) for k in range(8)]
        gate_ps, up_ps, turn_ps, out_ps = bank[0:2], bank[2:4], bank[4:6], bank[6:8]
        l1_ps, turnx_ps, turn1_ps, l2_ps = bank[0:4], bank[4], bank[5], bank[6:8]
        turnr_ps = turnx_ps[:, D:D + P]
        up3_ps, gate3_ps, turn3_ps, turnh_ps, out3_ps = bank[0], bank[1], bank[2], bank[3], bank[7]

        first_in = [sem(f"first_in{i}") for i in range(6)]
        first_hi, first_ready = sem("first_hi"), sem("first_ready")
        x_in_acc = sem("x_in_acc")
        cond_in, cond_wide_in = sem("cond_in"), sem("cond_wide_in")
        consts_made, bias_room, bias_in = sem("consts_made"), sem("bias_room"), sem("bias_in")
        zeros_made = sem("zeros_made")
        route_step = sem("route_step")
        route_max, route_exp, route_masks = sem("route_max"), sem("route_exp"), sem("route_masks")
        route_counts, route_slots, route_sums = sem("route_counts"), sem("route_slots"), sem("route_sums")
        route_read = sem("route_read")
        tables_ready = sem("tables_ready")
        raw_in = [sem(f"raw_in{k}") for k in range(NRAW)]
        raw_free = sem("raw_free")
        mask_in, masked = sem("mask_in"), sem("masked")
        split_step = sem("split_step")
        rows_step = sem("rows_step")
        biases_in = sem("biases_in")
        xraw_in = [sem(f"xraw_in{p}") for p in range(2)]
        xh_done, xl_done = sem("xh_done"), sem("xl_done")
        gate_done, up_done = sem("gate_done"), sem("up_done")
        gelu_done, hid_done, turn_done = sem("gelu_done"), sem("hid_done"), sem("turn_done")
        hh_done, hl_done = sem("hh_done"), sem("hl_done")
        down_done, acc_done = sem("down_done"), sem("acc_done")
        cross_done, x1_done, t1_done = sem("cross_done"), sem("x1_done"), sem("t1_done")
        x1h_done, x1l_done = sem("x1h_done"), sem("x1l_done")
        l1_done, mix_step, mix_last = sem("l1_done"), sem("mix_step"), sem("mix_last")
        mix_done = sem("mix_done")
        t2_done, x2h_done, x2l_done = sem("t2_done"), sem("x2h_done"), sem("x2l_done")
        base_done, ranks_done, turnr_done = sem("base_done"), sem("ranks_done"), sem("turnr_done")
        rh_done, rl_done, lora_done = sem("rh_done"), sem("rl_done"), sem("lora_done")
        kept_done = sem("kept_done")
        x3_done, spread_done = sem("x3_done"), sem("spread_done")
        gathered_done, t3_done = sem("gathered_done"), sem("t3_done")
        x3h_done, x3l_done, pick_done = sem("x3h_done"), sem("x3l_done"), sem("pick_done")
        up3_done, gate3_done = sem("up3_done"), sem("gate3_done")
        silu_done, hid3_done, turnh_done = sem("silu_done"), sem("hid3_done"), sem("turnh_done")
        h3h_done, h3l_done = sem("h3h_done"), sem("h3l_done")
        down3_done = sem("down3_done")
        y_done = sem("y_done")
        out_done = [sem(f"out_done{p}") for p in range(2)]

        block = ctx.enter_context(nc.Block())

        @block.sync
        def _(sp):
            def load_x(g, p, shared=False):
                for j in range(2):
                    if shared:
                        b = 2 * g + j
                    else:
                        b = sp.value_load(source0[0:1, bass.ds(2 * (g - NSH) + j, 1)], min_val=0, max_val=NB - 1)
                    dst = xraw[p].rearrange("p (c j s) -> p c j s", c=DC, j=2)[:, :, j, :]
                    sp.dma_start(dst, xT[bass.ds(b, 1)].rearrange("a p c s -> p (a c) s")).then_inc(xraw_in[p], 16)

            def home_x(pair):
                for j in range(2):
                    src = x.rearrange("(t j) s d -> t j s d", j=2)[bass.ds(2 * pair, 2), j]
                    sp.dma_start(acc[S * j:S * (j + 1), bass.ds(2 * pair, 2), :],
                                 src.rearrange("t s d -> s t d")).then_inc(x_in_acc, 16)

            def first_piece(i):
                sp.dma_start(first_raw[i], w0[0, :, i * PIECE:(i + 1) * PIECE]).then_inc(first_in[i], 16)

            sp.dma_start(condt, cond).then_inc(cond_in, 16)
            first_piece(0)
            load_x(0, 0, shared=True)
            for i in (1, 3, 4, 2):
                first_piece(i)
            load_x(1, 1, shared=True)
            first_piece(5)
            home_x(0)
            sp.wait_ge(xl_done, 1)
            load_x(2, 0, shared=True)
            home_x(1)
            sp.wait_ge(xl_done, 2)
            load_x(3, 1, shared=True)
            for j in range(2):
                sp.dma_start(Y1[S * j:S * (j + 1), :, :],
                             cond.rearrange("(t j) e -> j t e", j=2)[j:j + 1].broadcast_to([S, NSH, E]))\
                    .then_inc(cond_wide_in, 16)

            with sp.Fori(2, NSH // 2) as pair:
                for k in range(2):
                    g = 2 * pair + k
                    sp.wait_ge(xl_done, g - 1)
                    load_x(g, k, shared=True)
                    if k == 0:
                        home_x(pair)
            sp.wait_ge(tables_ready, 1)
            for dst, src in ((b1s, b1), (b2s, b2)):
                sp.dma_start(dst, src.rearrange("(a d) -> a d", a=1).broadcast_to([P, D])).then_inc(biases_in, 16)
            with sp.Fori(NSH // 2, G0 // 2) as pair:
                for k in range(2):
                    g = 2 * pair + k
                    sp.wait_ge(xl_done, g - 1)
                    load_x(g, k)

            with sp.Fori(0, G3 // 2) as pair:
                for k in range(2):
                    g = 2 * pair + k
                    sp.wait_ge(y_done, g + 1)
                    for j in range(2):
                        b = sp.value_load(dest3[0:1, bass.ds(2 * g + j, 1)], min_val=0, max_val=NB + SLOTS3 - 1)
                        sp.dma_start(out[bass.ds(b, 1)].rearrange("a s d -> (a s) d"),
                                     result[k][S * j:S * (j + 1), :]).then_inc(out_done[k], 16)
            for k in range(2):
                sp.wait_ge(out_done[k], 32 * (G3 // 2))

        @block.gpsimd
        def _(pool):
            def iota(dst, pattern, base, per_partition):
                return pool.iota(dst, pattern=pattern, base=base, channel_multiplier=per_partition,
                                 allow_small_or_imprecise_dtypes=True)

            iota(iota_slot, [[1, SLOTS0]], 0, 0)
            iota(small[:, 0:E], [[1, E]], -E, 0)
            iota(small[:, 8:9], [[0, 1]], -NONE, 1)
            pool.memset(tri, 1.0)
            pool.memset(one[:, :], 1.0)
            pool.memset(ones, 1.0)
            pool.memset(ident[:, :], 0.0)
            pool.memset(bias_raw, 0.0).then_inc(consts_made, 1)
            pool.wait_ge(consts_made, 1)
            pool.affine_select(out=tri, in_=tri, compare_op=ALU.is_gt, fill=0.0, base=0,
                               pattern=[[1, NB]], channel_multiplier=-1)
            pool.affine_select(out=ident[:, :], in_=ident[:, :], compare_op=ALU.not_equal, fill=1.0,
                               base=0, pattern=[[-1, P]], channel_multiplier=1).then_inc(consts_made, 1)

            def load(k, src):
                pool.dma_start(raw[:, k, :], src).then_inc(raw_in[k], 16)

            def split(k, step, at):
                hi, lo = Wh[:, at:at + PIECE], Wl[:, at:at + PIECE]
                pool.tensor_tensor(hi, raw[:, k, :], one[:, :].broadcast_to([P, PIECE]), ALU.mult)\
                    .then_inc(split_step, 1)
                pool.wait_ge(split_step, step + 1)
                pool.tensor_tensor(lo, raw[:, k, :], hi.bitcast(F32), ALU.subtract).then_inc(split_step, 1)
                pool.wait_ge(split_step, step + 2)
                pool.sem_inc(raw_free, 1)

            pool.wait_ge(first_in[5], 16)
            for q in range(2):
                at = bias_raw[32 * q:32 * q + E, :]
                pool.dma_start(at, b3).then_inc(bias_in, 16)
            pool.wait_ge(bias_in, 32)
            pool.tensor_tensor(rows3[:, :], bias_raw, one[0:64, :].broadcast_to([64, NBIAS]), ALU.mult)\
                .then_inc(rows_step, 1)
            pool.wait_ge(rows_step, 1)
            lo = rows3[32:64, :]
            pool.tensor_tensor(lo, bias_raw[32:64, :], lo.bitcast(F32), ALU.subtract).then_inc(rows_step, 1)
            pool.wait_ge(rows_step, 2)
            pool.wait_ge(first_ready, 6)
            pool.memset(acc[:, NSH:NB + 1, :], 0.0).then_inc(zeros_made, 1)

            def expert_at(chosen, turn, top):
                return pool.value_load(chosen[0:1, bass.ds(turn, 1)], min_val=0, max_val=top)

            def w0_piece(e, i):
                return w0[bass.ds(e, 1), :, i * PIECE:(i + 1) * PIECE].rearrange("a p n -> p (a n)")

            def expert(turn, slot, last=False, end=None):
                this = expert_at(chosen0, turn, E)
                after = None if last else expert_at(chosen0, turn + 1, E)
                if end is not None:
                    pool.wait_ge(down_done, end)
                for i in range(6):
                    k = i % NRAW
                    pool.wait_ge(raw_in[k], 32 * turn + 16 * (i // NRAW) + 16)
                    split(k, 12 * turn + 2 * i, slot * EXP0 + i * PIECE)
                    if i < NRAW:
                        load(k, w0_piece(this, i + NRAW))
                    elif not last:
                        load(k, w0_piece(after, i - NRAW))

            def expert_in_ring(turn, slot, last=False):
                expert(turn, slot, last,
                       end=pool.value_load(end0[0:1, bass.ds(turn - 2, 1)], min_val=2 * NSH, max_val=2 * G0))

            pool.wait_ge(tables_ready, 1)
            first_chosen = expert_at(chosen0, 0, E)
            for i in range(NRAW):
                load(i, w0_piece(first_chosen, i))
            expert(0, 1)
            pool.wait_ge(down_done, 2 * NSH)
            expert(1, 0)
            with pool.Fori(1, E // 2 - 1) as pair:
                expert_in_ring(2 * pair, 1)
                expert_in_ring(2 * pair + 1, 0)
            expert_in_ring(E - 2, 1)
            expert_in_ring(E - 1, 0, last=True)

            arrived = [32 * E] * NRAW
            srcs = [w1[:, n * PIECE:(n + 1) * PIECE] for n in range(4)] + [w2]
            pool.dma_start(maskt, mask).then_inc(mask_in, 16)
            for n in range(NRAW):
                load(n, srcs[n])
            pool.wait_ge(mask_in, 16)
            end = pool.value_load(end0[0:1, E - 2:E - 1], min_val=2 * NSH, max_val=2 * G0)
            pool.wait_ge(down_done, end)
            for n in range(5):
                k = n % NRAW
                arrived[k] += 16
                pool.wait_ge(raw_in[k], arrived[k])
                if n < 4:
                    m = maskt[:, (n // 2) * D:(n // 2 + 1) * D].unsqueeze(1).broadcast_to([P, 4, D])
                    r4 = raw[:, k, :].rearrange("p (g o) -> p g o", g=4)
                    pool.tensor_tensor(r4, r4, m, ALU.mult).then_inc(masked, 1)
                    pool.wait_ge(masked, n + 1)
                split(k, STEP12 + 2 * n, L1AT + n * PIECE)
                if n + NRAW < 5:
                    load(k, srcs[n + NRAW])

            def w3_piece(e, m):
                return w3[bass.ds(e, 1), :, m * PIECE:(m + 1) * PIECE].rearrange("a p n -> p (a n)")

            def expert3_in(turn, slot, last=False, end=None):
                after = None if last else expert_at(chosen3, turn + 1, E - 1)
                if end is not None:
                    pool.wait_ge(down3_done, end)
                for m in range(3):
                    k = (2 + m) % NRAW
                    pool.wait_ge(raw_in[k], arrived[k] + 16 * turn + 16)
                    split(k, STEP3 + 6 * turn + 2 * m, slot * EXP3 + m * PIECE)
                    if not last:
                        load(k, w3_piece(after, m))

            first_chosen3 = expert_at(chosen3, 0, E - 1)
            for m in range(3):
                load((2 + m) % NRAW, w3_piece(first_chosen3, m))
            pool.wait_ge(down_done, 2 * G0)
            expert3_in(0, 0)
            expert3_in(1, 1)
            pool.wait_ge(lora_done, NSH)
            expert3_in(2, 2)
            expert3_in(3, 3)
            for turn in range(4, E):
                expert3_in(turn, turn % 4, last=(turn == E - 1),
                           end=pool.value_load(end3[0:1, turn - 4:turn - 3], min_val=1, max_val=G3 + 1))

        @block.tensor
        def _(pe):
            def route_counts_():
                pe.wait_ge(consts_made, 2)
                pe.wait_ge(route_masks, 1)
                pe.wait_ge(hl_done, 3)
                both = small[:, 64:80]
                pe.matmul(turn_ps[0][0:NB, 0:16], tri, both, start=True, stop=True)
                pe.matmul(turn_ps[0][0:NB, 16:32], ones[:, 0:NB], both, start=True, stop=True).then_inc(route_counts, 1)

            def route_sums_():
                pe.wait_ge(route_slots, 1)
                pe.wait_ge(hl_done, 2 * FIRST - 1)
                colb = small[:, 8:9]
                pe.matmul(turn_ps[0][0:1, 0:SLOTS0], colb, T1, start=True, stop=True)
                pe.matmul(turn_ps[0][0:1, SLOTS0:SLOTS], colb, T3, start=True, stop=True)
                pe.matmul(turn_ps[0][:, SLOTS:SLOTS + SLOTS0], ones, TW, start=True, stop=True).then_inc(route_sums, 1)

            def product(ps, pairs):
                n = len(pairs)
                for i, (ah, al, bh, bl) in enumerate(pairs):
                    pe.matmul(ps, ah, bh, start=(i == 0), stop=False)
                    pe.matmul(ps, ah, bl, start=False, stop=False)
                    mm = pe.matmul(ps, al, bh, start=False, stop=(i == n - 1))
                return mm

            def chunk(t, c):
                return t[:, c * P:(c + 1) * P]

            def weights(at, n):
                return Wh[:, bass.ds(at, n)], Wl[:, bass.ds(at, n)]

            SHARED = -1

            def load_expert(g):
                return pe.value_load(turn0[0:1, bass.ds(g - NSH, 1)], min_val=0, max_val=E - 1)

            def up_gate(g, p, h, e, n2, first=False, xset=0):
                at = ((e + 1) % 2) * EXP0 + h * HALF0
                if h == 0:
                    pe.wait_ge(xl_done, g + 1)
                if not isinstance(e, int):
                    pe.wait_ge(split_step, 12 * e + 6 * h + 4)
                if not first:
                    pe.wait_ge(hid_done, n2 - 1)
                for ps, k, done in ((gate_ps[h], 0, gate_done), (up_ps[h], 1, up_done)):
                    if first:
                        pe.wait_ge(first_ready, 2 * h + k + 1)
                    product(ps[:, :], [(chunk(xh[xset][p], c), chunk(xl[xset][p], c),
                                        *weights(at + k * PIECE + c * 512, 512))
                                       for c in range(DC)]).then_inc(done, 1)

            def turn(h, n2, first=False):
                pe.wait_ge(hid_done, n2 + 1)
                if not first:
                    pe.wait_ge(hl_done, n2 - 1)
                for c in range(4):
                    mm = pe.transpose(chunk(turn_ps[h], c), chunk(hid[h], c), ident[:, :])
                mm.then_inc(turn_done, 1)

            def down(g, p, h, e, n2, first=False):
                at = ((e + 1) % 2) * EXP0 + h * HALF0 + 2 * PIECE
                pe.wait_ge(hl_done, n2 + 1)
                if not isinstance(e, int):
                    pe.wait_ge(split_step, 12 * e + 6 * h + 6)
                elif first:
                    pe.wait_ge(first_ready, 5 + h)
                if h == 0 and not first:
                    pe.wait_ge(acc_done, g - 1)
                ps = out_ps[p][:, 0:D]
                for c in range(4):
                    wh, wl = weights(at + c * D, D)
                    pe.matmul(ps, chunk(hh[h], c), wh, start=(h == 0 and c == 0), stop=False)
                    pe.matmul(ps, chunk(hh[h], c), wl, start=False, stop=False)
                    mm = pe.matmul(ps, chunk(hl[h], c), wh, start=False, stop=(h == 1 and c == 3))
                mm.then_inc(down_done, 1)

            def quarter_at(q, part):
                within = 2 * D if part == 2 else 2 * P
                return (q // 2) * HALF0 + part * PIECE + (q % 2) * within

            def two_groups(xset, lo_, c):
                t = XSET[xset].rearrange("p (g k n) -> p g k n", g=2, n=P)
                return t[:, :, DC * lo_ + c, :]

            def up_gate_shared(g, xset, q):
                n2 = 2 * g + q
                if q == 0:
                    pe.wait_ge(xl_done, g + 2)
                pe.wait_ge(hid_done, n2 - 1)
                for ps, part, done in ((gate_ps[q % 2], 0, gate_done), (up_ps[q % 2], 1, up_done)):
                    for j in range(2):
                        blocks = [quarter_at(q, part) + c * 512 + j * P for c in range(DC)]
                        dst = ps[:, 2 * P * j:2 * P * (j + 1)].rearrange("p (g n) -> p g n", g=2)
                        mm = product(dst, [(Wh[:, at:at + P], Wl[:, at:at + P],
                                            two_groups(xset, 0, c), two_groups(xset, 1, c))
                                           for c, at in enumerate(blocks)])
                    mm.then_inc(done, 1)

            def down_shared(g, q):
                n2 = 2 * g + q
                pe.wait_ge(hl_done, n2 + 1)
                if q == 0:
                    pe.wait_ge(acc_done, g)
                for p in range(2):
                    for j in range(2):
                        at, tokens = quarter_at(q, 2) + j * D, chunk(hh[q % 2], 2 * j + p)
                        tokens_lo = chunk(hl[q % 2], 2 * j + p)
                        ps = out_ps[p][:, 0:D]
                        pe.matmul(ps, tokens, Wh[:, at:at + D], start=(q == 0 and j == 0), stop=False)
                        pe.matmul(ps, tokens, Wl[:, at:at + D], start=False, stop=False)
                        mm = pe.matmul(ps, tokens_lo, Wh[:, at:at + D], start=False, stop=(q == 3 and j == 1))
                mm.then_inc(down_done, 1)

            def pair_shared(g, xset, first=False):
                up_gate_shared(g, xset, 0)
                if first:
                    turn(1, 2 * g - 1)
                    down(g - 1, 1, 0, SHARED, 2 * g - 2)
                else:
                    down_shared(g - 2, 2)
                up_gate_shared(g, xset, 1)
                if first:
                    down(g - 1, 1, 1, SHARED, 2 * g - 1)
                else:
                    down_shared(g - 2, 3)
                for q in (2, 3):
                    up_gate_shared(g, xset, q)
                    down_shared(g, q - 2)

            def group(g, p, n=3, e=None, before=None, xset=1, after_shared=False):
                e = load_expert(g) if e is None else e
                up_gate(g, p, 0, e, 2 * g, first=n < 1, xset=xset)
                if after_shared:
                    down_shared(g - 2, 2)
                elif n > 0:
                    before = load_expert(g - 1) if before is None else before
                    turn(1, 2 * g - 1, first=n < 2)
                    down(g - 1, 1 - p, 0, before, 2 * g - 2, first=n < 3)
                up_gate(g, p, 1, e, 2 * g + 1, first=n < 1, xset=xset)
                if n == 2:
                    pe.wait_ge(route_read, 1)
                turn(0, 2 * g, first=n < 1)
                if after_shared:
                    down_shared(g - 2, 3)
                elif n > 0:
                    down(g - 1, 1 - p, 1, before, 2 * g - 1, first=n < 3)

            pe.wait_ge(consts_made, 2)
            with pe.Fori(0, WARM_UP):
                pe.matmul(out_ps[1][:, 0:P], ident[:, :], ident[:, :], start=True, stop=True)
            group(0, 0, n=0, e=SHARED, xset=0)
            group(1, 1, n=1, e=SHARED, before=SHARED, xset=0)
            route_counts_()
            group(2, 0, n=2, e=SHARED, before=SHARED, xset=0)
            group(3, 1, e=SHARED, before=SHARED, xset=0)
            route_sums_()
            pair_shared(FIRST, 1, first=True)
            with pe.Fori(0, (NSH - FIRST - 4) // 4) as four:
                pair_shared(4 * four + FIRST + 2, 0)
                pair_shared(4 * four + FIRST + 4, 1)
            pair_shared(NSH - 2, 0)
            pe.wait_ge(tables_ready, 1)
            group(NSH, 0, after_shared=True)
            group(NSH + 1, 1)
            with pe.Fori(NSH // 2 + 1, G0 // 2) as pair:
                group(2 * pair, 0)
                group(2 * pair + 1, 1)
            last = load_expert(G0 - 1)
            turn(1, 2 * G0 - 1)
            down(G0 - 1, 1, 0, last, 2 * G0 - 2)
            down(G0 - 1, 1, 1, last, 2 * G0 - 1)

            def turn_x(t, ps):
                for c in range(DC):
                    mm = pe.transpose(chunk(ps, c), chunk(t, c), ident[:, :])
                return mm

            def turn_x1(i, p, first=False):
                pe.wait_ge(x1_done, i + 1)
                if first:
                    pe.wait_ge(hl_done, 2 * G0)
                else:
                    pe.wait_ge(x1l_done, i)
                turn_x(x1[p], turn1_ps).then_inc(t1_done, 1)

            def layer1(i, p, k, first=False):
                if k == 0:
                    pe.wait_ge(x1l_done, i + 1)
                if not first:
                    if k < 3:
                        pe.wait_ge(mix_step, 8 * i + 2 * k - 5)
                    else:
                        pe.wait_ge(mix_done, i)
                at = [L1AT + c * E * D + k * 512 for c in range(DC)]
                product(l1_ps[k][:, :], [(chunk(x1h[p], c), chunk(x1l[p], c), Wh[:, at[c]:at[c] + 512],
                                          Wl[:, at[c]:at[c] + 512]) for c in range(DC)]).then_inc(l1_done, 1)

            def base(i, p, first=False):
                pe.wait_ge(x2l_done, i + 1)
                if not first:
                    pe.wait_ge(x3_done, i - 1)
                n = D + E * R
                at = [L2AT + c * n for c in range(DC)]
                product(l2_ps[p][:, 0:n], [(chunk(x2h[p], c), chunk(x2l[p], c), Wh[:, at[c]:at[c] + n],
                                         Wl[:, at[c]:at[c] + n]) for c in range(DC)]).then_inc(base_done, 1)

            def turn_ranks(i, first=False):
                pe.wait_ge(ranks_done, i + 1)
                if not first:
                    pe.wait_ge(rl_done, i)
                pe.transpose(turnr_ps, ranks, ident[:, :]).then_inc(turnr_done, 1)

            def lora(i, p):
                pe.wait_ge(rl_done, i + 1)
                at = L2AT + 3 * D
                for ah, w in ((rh, Wh), (rh, Wl), (rl, Wh)):
                    mm = pe.matmul(l2_ps[p][:, 0:D], ah, w[:, at:at + D], start=False, stop=(ah is rl),
                                   skip_group_check=True)
                mm.then_inc(lora_done, 1)

            def turn_x2(i, p, first=False):
                pe.wait_ge(mix_done, i + 1)
                if not first:
                    pe.wait_ge(x2l_done, i)
                turn_x(x2[p], turnx_ps).then_inc(t2_done, 1)

            pe.sem_inc(down3_done, 1)
            turn_x1(0, 0, first=True)
            pe.wait_ge(split_step, STEP3)
            pe.wait_ge(acc_done, G0)

            def step(i, p, before=True, after=True, first=False, second=False, third=False):
                layer1(i, p, 0, first=first)
                layer1(i, p, 1, first=first)
                if before and not second:
                    lora(i - 2, p)
                if before:
                    turn_x2(i - 1, 1 - p, first=second)
                if after:
                    turn_x1(i + 1, 1 - p)
                layer1(i, p, 2, first=first)
                if before:
                    base(i - 1, 1 - p, first=second or third)
                layer1(i, p, 3, first=first)
                if before:
                    turn_ranks(i - 1, first=second)

            step(0, 0, before=False, first=True)
            step(1, 1, second=True)
            step(2, 0, third=True)
            step(3, 1)
            with pe.Fori(2, NSH // 2 - 1) as pair:
                step(2 * pair, 0)
                step(2 * pair + 1, 1)
            step(NSH - 2, 0)
            step(NSH - 1, 1, after=False)
            lora(NSH - 2, 0)
            turn_x2(NSH - 1, 1)
            base(NSH - 1, 1)
            turn_ranks(NSH - 1)
            lora(NSH - 1, 1)

            def turn_x3(i, p, first=False):
                pe.wait_ge(gathered_done, i + 1)
                if first:
                    pe.wait_ge(mix_done, NSH)
                else:
                    pe.wait_ge(x3l_done, i)
                turn_x(gathered[p], turn3_ps).then_inc(t3_done, 1)

            def load_expert3(i):
                return pe.value_load(turn3[0:1, bass.ds(i, 1)], min_val=0, max_val=E - 1)

            def up_gate3(i, p, e, first=False):
                at = (e % 4) * EXP3
                pe.wait_ge(x3l_done, i + 1)
                pe.wait_ge(split_step, STEP3 + 6 * e + 4)
                if not first:
                    pe.wait_ge(hid3_done, i)
                for ps, k, done in ((up3_ps, 0, up3_done), (gate3_ps, 1, gate3_done)):
                    for c in range(DC):
                        wh, wl = weights(at + k * PIECE + c * 512, 512)
                        pe.matmul(ps[:, :], chunk(x3h, c), wh, start=(c == 0), stop=False)
                        pe.matmul(ps[:, :], chunk(x3h, c), wl, start=False, stop=False)
                        pe.matmul(ps[:, :], chunk(x3l, c), wh, start=False, stop=False)
                    if k == 0:
                        pe.wait_ge(pick_done, i + 1)
                    pe.matmul(ps[:, :], pick3[:, p, :], rows3[:, k * I3:(k + 1) * I3], start=False, stop=True)\
                        .then_inc(done, 1)

            def turn_h(i, first=False):
                pe.wait_ge(hid3_done, i + 1)
                if not first:
                    pe.wait_ge(h3l_done, i)
                for c in range(4):
                    mm = pe.transpose(chunk(turnh_ps, c), chunk(hid3, c), ident[:, :])
                mm.then_inc(turnh_done, 1)

            def down3(i, p, e, first=False):
                at = (e % 4) * EXP3 + 2 * PIECE
                pe.wait_ge(h3l_done, i + 1)
                pe.wait_ge(split_step, STEP3 + 6 * e + 6)
                if not first:
                    pe.wait_ge(y_done, i)
                ps = out3_ps[:, 0:D]
                pe.matmul(ps, pick3[:, p, :], rows3[:, 2 * I3:2 * I3 + D], start=True, stop=False)
                for c in range(4):
                    wh, wl = weights(at + c * D, D)
                    pe.matmul(ps, chunk(h3h, c), wh, start=False, stop=False)
                    pe.matmul(ps, chunk(h3h, c), wl, start=False, stop=False)
                    mm = pe.matmul(ps, chunk(h3l, c), wh, start=False, stop=(c == 3))
                mm.then_inc(down3_done, 1)

            def step3(i, p, before=True, after=True, after2=True, first=False, second=False):
                if before:
                    e_before = load_expert3(i - 1)
                if after:
                    e_after = load_expert3(i + 1)
                if before:
                    down3(i - 1, 1 - p, e_before, first=second)
                turn_h(i, first=first)
                if after:
                    up_gate3(i + 1, 1 - p, e_after)
                if after2:
                    turn_x3(i + 2, p)

            turn_x3(0, 0, first=True)
            pe.wait_ge(rows_step, 2)
            up_gate3(0, 0, load_expert3(0), first=True)
            turn_x3(1, 1)
            step3(0, 0, before=False, first=True)
            step3(1, 1, second=True)
            with pe.Fori(1, G3 // 2 - 1) as pair:
                step3(2 * pair, 0)
                step3(2 * pair + 1, 1)
            step3(G3 - 2, 0, after2=False)
            step3(G3 - 1, 1, after=False, after2=False)
            down3(G3 - 1, 1, load_expert3(G3 - 1))

        @block.scalar
        def _(act):
            act.wait_ge(route_max, 1)
            act.activation(small[:, 32:40], condt, ACT.Exp, bias=small[:, 17:18],
                           accum_out=small[:, 18:19]).then_inc(route_exp, 1)
            act.activation(small[:, 283:284], condt[:, 0:1], ACT.Gelu_apprx_tanh)

            def split_x(g, p, free=None, xset=1):
                act.wait_ge(xraw_in[p], 16 * (g - p) + 32)
                if free is not None:
                    act.wait_ge(up_done, free)
                act.activation(xh[xset][p], xraw[p], ACT.Copy).then_inc(xh_done, 1)

            def gelu(h, n2, first=False):
                act.wait_ge(gate_done, n2 + 1)
                if not first:
                    act.wait_ge(hid_done, n2 - 1)
                act.activation(gl[h], gate_ps[h][:, :], ACT.Gelu_apprx_tanh).then_inc(gelu_done, 1)

            def hidden_hi(h, n2, first=False, skipped=0):
                act.wait_ge(turn_done, n2 + 1 - skipped)
                if not first:
                    act.wait_ge(down_done, n2 - 1)
                act.activation(hh[h], turn_ps[h][:, :], ACT.Copy).then_inc(hh_done, 1)

            def hidden_hi_shared(h, n2):
                act.wait_ge(hid_done, n2 + 1)
                act.wait_ge(down_done, n2 - 1)
                act.activation(hh[h], hid[h], ACT.Copy).then_inc(hh_done, 1)

            def pair_shared(g, xset, first=False, last=False):
                gelu(0, 2 * g)
                if first:
                    hidden_hi(1, 2 * g - 1)
                else:
                    hidden_hi_shared(1, 2 * g - 1)
                for p in range(1 if last else 2):
                    split_x(g + 2 + p, p, free=2 * g, xset=1 - xset)
                for q in range(1, 4):
                    gelu(q % 2, 2 * g + q)
                    hidden_hi_shared((q - 1) % 2, 2 * g + q - 1)

            def group(g, p, n=3, after=1, skipped=TURNLESS, xset=1, after_shared=False):
                gelu(0, 2 * g, first=n < 1)
                if after_shared:
                    hidden_hi_shared(1, 2 * g - 1)
                elif n > 0:
                    hidden_hi(1, 2 * g - 1, first=n < 2, skipped=skipped)
                if after == 1:
                    split_x(g + 1, 1 - p, free=None if n < 1 else 2 * g, xset=xset)
                elif after == 2:
                    for k in range(2):
                        split_x(g + 1 + k, k)
                gelu(1, 2 * g + 1, first=n < 1)
                hidden_hi(0, 2 * g, first=n < 1, skipped=skipped)

            def first_piece(i):
                act.wait_ge(first_in[i], 16)
                act.activation(Wh[:, i * PIECE:(i + 1) * PIECE], first_raw[i], ACT.Copy).then_inc(first_hi, 1)

            first_piece(0)
            split_x(0, 0, xset=0)
            for i in (1, 3, 4):
                first_piece(i)
            gelu(0, 0, first=True)
            first_piece(2)
            split_x(1, 1, xset=0)
            first_piece(5)
            gelu(1, 1, first=True)
            hidden_hi(0, 0, first=True)
            group(1, 1, n=1, skipped=0, xset=0)
            group(2, 0, skipped=0, xset=0)
            group(3, 1, skipped=0, after=2)
            pair_shared(FIRST, 1, first=True)
            with act.Fori(0, (NSH - FIRST - 4) // 4) as four:
                pair_shared(4 * four + FIRST + 2, 0)
                pair_shared(4 * four + FIRST + 4, 1)
            pair_shared(NSH - 2, 0, last=True)
            group(NSH, 0, after_shared=True)
            group(NSH + 1, 1)
            with act.Fori(NSH // 2 + 1, G0 // 2 - 1) as pair:
                group(2 * pair, 0)
                group(2 * pair + 1, 1)
            group(G0 - 2, 0)
            group(G0 - 1, 1, after=0)
            hidden_hi(1, 2 * G0 - 1, skipped=TURNLESS)

            def hi(arrived, count, dst, src, done, free=None, freed=None):
                act.wait_ge(arrived, count)
                if free is not None:
                    act.wait_ge(free, freed)
                act.activation(dst, src, ACT.Copy).then_inc(done, 1)

            def at_place(t, half, b):
                return t[half, bass.ds(b, 1), :].rearrange("p a d -> p (a d)")

            halves = (slice(0, S), slice(S, P))

            def cross_over(i, first=False):
                if not first:
                    act.wait_ge(x1_done, i)
                for j in range(2):
                    op = act.activation(cross[halves[j], :], at_place(acc, halves[1 - j], NSH + i), ACT.Copy)
                op.then_inc(cross_done, 1)

            def spread(i):
                act.wait_ge(x3_done, i + 1)
                for j in range(2):
                    op = act.activation(at_place(acc, halves[1 - j], NSH + i), at_place(acc, halves[j], i), ACT.Copy)
                op.then_inc(spread_done, 1)

            def step(i, p, before=True, after=True, after2=True, first=False, second=False, third=False):
                if before and not second:
                    hi(turnr_done, i - 1, rh, turnr_ps, rh_done,
                       *((None, None) if third else (lora_done, i - 2)))
                if after2:
                    cross_over(i + 2)
                if before:
                    hi(t2_done, i, x2h[1 - p], turnx_ps[:, 0:D], x2h_done,
                       *((None, None) if second or third else (base_done, i - 2)))
                if after:
                    hi(t1_done, i + 2, x1h[1 - p], turn1_ps[:, 0:D], x1h_done,
                       *((None, None) if first else (l1_done, 4 * i)))
                if before and not second:
                    spread(i - 2)

            act.wait_ge(acc_done, G0)
            cross_over(0, first=True)
            cross_over(1)
            hi(t1_done, 1, x1h[0], turn1_ps[:, 0:D], x1h_done)
            step(0, 0, before=False, first=True)
            step(1, 1, second=True)
            step(2, 0, third=True)
            step(3, 1)
            with act.Fori(2, NSH // 2 - 1) as pair:
                step(2 * pair, 0)
                step(2 * pair + 1, 1)
            step(NSH - 2, 0, after2=False)
            step(NSH - 1, 1, after=False, after2=False)
            hi(turnr_done, NSH - 1, rh, turnr_ps, rh_done, lora_done, NSH - 2)
            hi(t2_done, NSH, x2h[1], turnx_ps[:, 0:D], x2h_done, base_done, NSH - 2)
            hi(turnr_done, NSH, rh, turnr_ps, rh_done, lora_done, NSH - 1)
            spread(NSH - 2)
            spread(NSH - 1)

            def gather(i, p, first=False):
                batches = [act.value_load(place[0:1, bass.ds(SLOTS0 + 2 * i + j, 1)], min_val=0, max_val=NONE)
                           for j in range(2)]
                if first:
                    act.wait_ge(spread_done, NSH)
                else:
                    act.wait_ge(t3_done, i - 1)
                for j, b in enumerate(batches):
                    op = act.activation(gathered[p][halves[j], :], at_place(acc, halves[j], b), ACT.Copy)
                op.then_inc(gathered_done, 1)

            def pick(i, p, first=False):
                if not first:
                    act.wait_ge(down3_done, i)
                act.activation(pick3[:, p, :], is3[:, bass.ds(i, 1)].broadcast_to([64, P]), ACT.Copy)\
                    .then_inc(pick_done, 1)

            def silu(i, first=False):
                act.wait_ge(up3_done, i + 1)
                if not first:
                    act.wait_ge(hid3_done, i)
                act.activation(act3, up3_ps[:, :], ACT.Silu).then_inc(silu_done, 1)

            def step3(i, p, before=True, after=True, after2=True, first=False, second=False):
                if before:
                    hi(turnh_done, i, h3h, turnh_ps[:, :], h3h_done,
                       *((None, None) if second else (down3_done, i)))
                if after2:
                    gather(i + 2, p)
                silu(i, first=first)
                if after:
                    hi(t3_done, i + 2, x3h, turn3_ps[:, 0:D], x3h_done, gate3_done, i + 1)
                    pick(i + 1, 1 - p, first=first)

            for i in range(2):
                gather(i, i, first=True)
            hi(t3_done, 1, x3h, turn3_ps[:, 0:D], x3h_done)
            pick(0, 0, first=True)
            step3(0, 0, before=False, first=True)
            step3(1, 1, second=True)
            with act.Fori(1, G3 // 2 - 1) as pair:
                step3(2 * pair, 0)
                step3(2 * pair + 1, 1)
            step3(G3 - 2, 0, after2=False)
            step3(G3 - 1, 1, after=False, after2=False)
            hi(turnh_done, G3, h3h, turnh_ps[:, :], h3h_done, down3_done, G3)

        @block.vector
        def _(dve):
            count = [0]

            def done(op):
                count[0] += 1
                op.then_inc(route_step, 1)
                dve.wait_ge(route_step, count[0])

            TT, TS, STT = dve.tensor_tensor, dve.tensor_scalar, dve.scalar_tensor_tensor
            eid = small[:, 0:E]
            colb = small[:, 8:9]
            def col(k):
                return small[:, k:k + 1]
            m1, i1, m2, i2, nm1, ssum, w1c, w2c, rc, pos1, pos2, pos3 = (
                col(k) for k in (16, 19, 20, 21, 17, 18, 22, 23, 24, 25, 26, 27))
            ex, junk = small[:, 32:40], small[:, 40:48]
            M1, M2 = small[:, 48:56], small[:, 56:64]
            both = small[:, 64:80].rearrange("b (a e) -> b a e", a=2)
            Mt, M3 = both[:, 0, :], both[:, 1, :]
            cond2 = small[:, 80:88]

            def first_of(values, top, index, mask):
                done(TS(junk, values, top, None, ALU.is_ge))
                done(TT(junk, junk, eid, ALU.mult))
                done(dve.tensor_reduce(index, junk, AX.X, ALU.min))
                done(TS(mask, eid, index, None, ALU.is_equal))

            def route_choose():
                dve.wait_ge(cond_in, 16)
                done(dve.tensor_reduce(m1, condt, AX.X, ALU.max))
                TS(nm1, m1, -1.0, None, ALU.mult).then_inc(route_max, 1)
                dve.wait_ge(consts_made, 2)
                first_of(condt, m1, i1, M1)
                done(STT(cond2, M1, -3.0e38, condt, ALU.mult, ALU.add))
                done(dve.tensor_reduce(m2, cond2, AX.X, ALU.max))
                first_of(cond2, m2, i2, M2)
                TT(Mt, M1, M2, ALU.add)
                dve.tensor_copy(M3, M1).then_inc(route_masks, 1)

            def blocks(k):
                return small[:, k:k + 16].rearrange("b (a e) -> b a e", a=2)

            def route_weights():
                dve.wait_ge(route_exp, 1)
                done(dve.reciprocal(rc, ssum))
                done(TS(ex, ex, rc, None, ALU.mult))
                for m, w in ((M1, w1c), (M2, w2c)):
                    done(TT(junk, ex, m, ALU.mult))
                    done(dve.tensor_reduce(w, junk, AX.X, ALU.add))
                done(TT(rc, w1c, w2c, ALU.add))
                done(dve.reciprocal(rc, rc))
                for w in (w1c, w2c):
                    done(TT(w, w, rc, ALU.mult))
                    done(TS(col(28), w, TOP_SCALE, None, ALU.mult))
                    done(STT(w, w, 1.0 - TOP_SCALE, col(28), ALU.mult, ALU.add))

            groups, sum1, sum2, ends, begins, places = (blocks(k) for k in (104, 120, 136, 152, 168, 184))
            present, turns = blocks(248), blocks(264)
            counts = small[:, 200:232]

            def running_sums(first, last):
                for a, b, k in ((first, sum1, 1), (sum1, sum2, 2), (sum2, last, 4)):
                    dve.tensor_copy(b[:, :, 0:k], a[:, :, 0:k])
                    done(TT(b[:, :, k:E], a[:, :, k:E], a[:, :, 0:E - k], ALU.add))

            def route_read_counts():
                dve.wait_ge(route_counts, 1)
                dve.tensor_copy(counts, turn_ps[0][0:NB, 0:32]).then_inc(route_read, 1)
                dve.wait_ge(route_read, 1)

            def route_places():
                ints = small[:, 88:104].bitcast(I32)
                done(TS(ints, counts[:, 16:32], 1.0, None, ALU.add))
                done(TS(ints, ints, 1, None, ALU.logical_shift_right))
                done(dve.tensor_copy(groups, ints.rearrange("b (a e) -> b a e", a=2)))
                running_sums(groups, ends)
                done(TT(begins, ends, groups, ALU.subtract))
                done(STT(places, begins, 2.0, counts[:, 0:16].rearrange("b (a e) -> b a e", a=2), ALU.mult, ALU.add))
                for m, a, pos in ((M1, 0, pos1), (M2, 0, pos2), (M1, 1, pos3)):
                    done(TT(junk, places[:, a, :], m, ALU.mult))
                    done(dve.tensor_reduce(pos, junk, AX.X, ALU.add))
                TS(T1, iota_slot, pos1, None, ALU.is_equal)
                TS(T3, iota_slot[:, 0:SLOTS3], pos3, None, ALU.is_equal)
                done(TS(T2, iota_slot, pos2, None, ALU.is_equal))
                done(TS(TW, T1, w1c, None, ALU.mult))
                done(STT(TW, T2, w2c, TW, ALU.mult, ALU.add))
                TT(T1, T1, T2, ALU.add).then_inc(route_slots, 1)

            def route_turns():
                done(TS(present, groups, 0.0, None, ALU.is_gt))
                running_sums(present, turns)
                done(TT(turns, turns, present, ALU.subtract))
                picks, terms = (passed[:, k:k + E * E].rearrange("b (t e) -> b t e", t=E) for k in (0, E * E))

                def by_turn(t):
                    return t.unsqueeze(1).broadcast_to([NB, E, E])

                for a, n in ((0, NR0), (1, G3)):
                    done(TT(picks, by_turn(turns[:, a, :]), iota_slot[:, 0:E].unsqueeze(2).broadcast_to([NB, E, E]),
                            ALU.is_equal))
                    done(TT(picks, picks, by_turn(present[:, a, :]), ALU.mult))
                    done(TT(terms, picks, by_turn(eid), ALU.mult))
                    done(dve.tensor_reduce(begins[:, a, :], terms, AX.X, ALU.add))
                    done(TS(junk, ends[:, a, :], float(-n), None, ALU.add))
                    done(TT(terms, picks, by_turn(junk), ALU.mult))
                    done(dve.tensor_reduce(places[:, a, :], terms, AX.X, ALU.add))
                TS(chosen0[:, :], begins[0:1, 0, :], float(E + 1), float(E), ALU.add, ALU.min)
                TS(chosen3[:, :], begins[0:1, 1, :], float(E), float(E - 1), ALU.add, ALU.min)
                TS(end0[:, :], places[0:1, 0, :], float(NR0 + NSH), 2.0, ALU.add, ALU.mult)
                done(TS(end3[:, :], places[0:1, 1, :], float(G3 + 1), None, ALU.add))

            def route_experts():
                for a, n, turn_of in ((0, NR0, turn0), (1, G3, turn3)):
                    v = passed[:, 0:n * (E - 1)].rearrange("b (n k) -> b n k", n=n)
                    done(TT(v, iota_slot[:, 0:n].unsqueeze(2).broadcast_to([NB, n, E - 1]),
                            ends[:, a, 0:E - 1].unsqueeze(1).broadcast_to([NB, n, E - 1]), ALU.is_ge))
                    if a == 1:
                        done(dve.tensor_reduce(expert_of, v, AX.X, ALU.add))
                    done(TT(v, v, present[:, a, 0:E - 1].unsqueeze(1).broadcast_to([NB, n, E - 1]), ALU.mult))
                    done(dve.tensor_reduce(ended[:, 0:n], v, AX.X, ALU.add))
                    done(dve.tensor_copy(turn_of[:, :], ended[0:1, 0:n]))
                row, row32 = col(9), col(10)
                done(TS(row, colb, float(NONE), None, ALU.add))
                done(TS(row32, row, 32.0, -32.0, ALU.is_ge, ALU.mult))
                done(TT(row32, row, row32, ALU.add))
                done(TS(is3[:, :], expert_of, row32, None, ALU.is_equal))

            def route_tables():
                dve.wait_ge(route_sums, 1)
                done(dve.tensor_copy(slot_row, iota_slot[0:1, 0:SLOTS3]))
                batch, flag, part = (tab[k] for k in range(3))
                whole, odd = (tab[k].bitcast(I32) for k in (3, 4))
                for j in range(2):
                    half = slice(S * j, S * (j + 1))
                    dve.tensor_copy(weight0[half, :], turn_ps[0][half, SLOTS + j:SLOTS + SLOTS0:2])
                TS(batch, turn_ps[0][0:1, 0:SLOTS], float(NONE), None, ALU.add).then_inc(route_read, 1)
                dve.wait_ge(route_read, 2)
                TS(source0[:, :], batch[:, 0:SLOTS0], float(NB - 1), None, ALU.min)
                done(dve.tensor_copy(whole, batch))
                done(TS(odd, whole, 1, None, ALU.bitwise_and))
                done(TS(whole, whole, 1, None, ALU.logical_shift_right))
                for j in range(2):
                    op = TS(flag[:, j::2], odd[:, j::2], float(j), float(NSH), ALU.not_equal, ALU.mult)
                done(op)
                done(TT(part, whole, flag, ALU.add))
                done(TS(flag, batch, float(NONE), float(NB), ALU.is_ge, ALU.mult))
                done(TT(part, part, flag, ALU.add))
                TS(place[:, :], part, float(NONE), None, ALU.min)
                b3_, f3 = batch[:, SLOTS0:SLOTS], flag[:, SLOTS0:SLOTS]
                done(TS(f3, f3, 1.0 / NB, None, ALU.mult))
                done(TT(f3, f3, slot_row[:, :], ALU.mult))
                TT(dest3[:, :], b3_, f3, ALU.add).then_inc(tables_ready, 1)

            def split_x(g, p, xset=1):
                dve.wait_ge(xh_done, g + 1)
                TT(xl[xset][p], xraw[p], xh[xset][p].bitcast(F32), ALU.subtract).then_inc(xl_done, 1)

            def hidden(h, n2, turned=None):
                dve.wait_ge(gelu_done, n2 + 1)
                dve.wait_ge(up_done, n2 + 1)
                if turned is not None:
                    dve.wait_ge(turn_done, turned)
                elif not (isinstance(n2, int) and n2 < 2):
                    dve.wait_ge(hl_done, n2 - 1)
                TT(hid[h], up_ps[h][:, :], gl[h], ALU.mult).then_inc(hid_done, 1)

            def hidden_lo(h, n2):
                dve.wait_ge(hh_done, n2 + 1)
                TT(hl[h], turn_ps[h][:, :], hh[h].bitcast(F32), ALU.subtract).then_inc(hl_done, 1)

            def hidden_lo_shared(h, n2):
                dve.wait_ge(hh_done, n2 + 1)
                TT(hl[h], hid[h], hh[h].bitcast(F32), ALU.subtract).then_inc(hl_done, 1)

            def add_shared(g, p, pairs=False):
                dve.wait_ge(down_done, 2 * (g - p) + 4 if pairs else 2 * g + 2)
                dve.wait_ge(x_in_acc, 16 * (g - p) + 32)
                at = acc[:, bass.ds(g, 1), :].rearrange("p a d -> p (a d)")
                TT(at, out_ps[p][:, 0:D], at, ALU.add).then_inc(acc_done, 1)

            def add_pair(g):
                for p in range(2):
                    add_shared(g + p, p, pairs=True)

            def pair_shared(g, xset, first=False, last=False):
                hidden(0, 2 * g, turned=2 * g - 1 if first else None)
                if first:
                    hidden_lo(1, 2 * g - 1)
                else:
                    hidden_lo_shared(1, 2 * g - 1)
                for p in range(1 if last else 2):
                    split_x(g + 2 + p, p, xset=1 - xset)
                for q in range(1, 4):
                    hidden(q % 2, 2 * g + q, turned=2 * g if first and q == 1 else None)
                    hidden_lo_shared((q - 1) % 2, 2 * g + q - 1)
                    if q == 1:
                        if first:
                            add_shared(g - 1, 1)
                        else:
                            add_pair(g - 2)

            def add(g, p):
                batches = [dve.value_load(place[0:1, bass.ds(2 * (g - NSH) + j, 1)], min_val=0, max_val=NONE)
                           for j in range(2)]
                dve.wait_ge(down_done, 2 * g + 2)
                dve.wait_ge(acc_done, g)
                for j, b in enumerate(batches):
                    half = slice(S * j, S * (j + 1))
                    at = acc[half, bass.ds(b, 1), :].rearrange("p a d -> p (a d)")
                    op = STT(at, out_ps[p][half, 0:D], weight0[half, bass.ds(g - NSH, 1)], at, ALU.mult, ALU.add)
                op.then_inc(acc_done, 1)

            def group(g, p, n=3, after=1, add_before=add, skipped=TURNLESS, xset=1, after_shared=False):
                for h in range(2):
                    hidden(h, 2 * g + h, turned=None if after_shared or n < 1 else 2 * g + h - 1 - skipped)
                    if h == 0:
                        if after_shared:
                            hidden_lo_shared(1, 2 * g - 1)
                        elif n > 0:
                            hidden_lo(1, 2 * g - 1)
                        if after == 1:
                            split_x(g + 1, 1 - p, xset=xset)
                        elif after == 2:
                            for k in range(2):
                                split_x(g + 1 + k, k)
                    else:
                        hidden_lo(0, 2 * g)
                if after_shared:
                    add_pair(g - 2)
                elif n > 0:
                    add_before(g - 1, 1 - p)

            def first_piece(n, i):
                dve.wait_ge(first_hi, n)
                TT(Wl[:, i * PIECE:(i + 1) * PIECE], first_raw[i], Wh[:, i * PIECE:(i + 1) * PIECE].bitcast(F32),
                   ALU.subtract).then_inc(first_ready, 1)

            route_choose()
            first_piece(1, 0)
            split_x(0, 0, xset=0)
            for n, i in enumerate((1, 3, 4)):
                first_piece(n + 2, i)
            hidden(0, 0)
            first_piece(5, 2)
            split_x(1, 1, xset=0)
            first_piece(6, 5)
            hidden(1, 1)
            hidden_lo(0, 0)
            group(1, 1, n=1, add_before=add_shared, skipped=0, xset=0)
            route_read_counts()
            route_weights()
            group(2, 0, add_before=add_shared, skipped=0, xset=0)
            route_places()
            group(3, 1, add_before=add_shared, skipped=0, after=2)
            route_turns()
            pair_shared(FIRST, 1, first=True)
            route_experts()
            pair_shared(FIRST + 2, 0)
            pair_shared(FIRST + 4, 1)
            route_tables()
            with dve.Fori(1, (NSH - FIRST - 4) // 4) as four:
                pair_shared(4 * four + FIRST + 2, 0)
                pair_shared(4 * four + FIRST + 4, 1)
            pair_shared(NSH - 2, 0, last=True)
            group(NSH, 0, after_shared=True)
            dve.wait_ge(zeros_made, 1)
            group(NSH + 1, 1)
            with dve.Fori(NSH // 2 + 1, G0 // 2 - 1) as pair:
                group(2 * pair, 0)
                group(2 * pair + 1, 1)
            group(G0 - 2, 0)
            group(G0 - 1, 1, after=0)
            hidden_lo(1, 2 * G0 - 1)
            add(G0 - 1, 1)

            def home(i):
                return acc[:, bass.ds(i, 1), :].rearrange("p a d -> p (a d)")

            def join(i, p, first=False):
                dve.wait_ge(cross_done, i + 1)
                if first:
                    dve.wait_ge(acc_done, G0)
                else:
                    dve.wait_ge(t1_done, i - 1)
                TT(x1[p], cross, home(i), ALU.add).then_inc(x1_done, 1)

            def mix_start(i, p, first=False):
                if not first:
                    dve.wait_ge(t2_done, i - 1)
                    dve.wait_ge(kept_done, i - 1)
                TT(x2[p], x1[p], b1s, ALU.add).then_inc(mix_step, 1)

            def mix(i, p, k):
                for q in range(2):
                    y = Y1[:, bass.ds(i, 1), 2 * k + q]
                    ps = l1_ps[k][:, q * D:(q + 1) * D]
                    if k == 0 and q == 0:
                        dve.wait_ge(l1_done, 4 * i + 1)
                        dve.wait_ge(mix_step, 8 * i + 1)
                    if k == 0 and q == 1:
                        TS(mixed, ps, y, None, ALU.mult).then_inc(mix_step, 1)
                        return
                    if q == 0:
                        dve.wait_ge(l1_done, 4 * i + k + 1)
                    if k < 3:
                        sum_ = (x2[p], mixed)[q]
                        if k > 0:
                            dve.wait_ge(mix_step, 8 * i + 2 * k + q)
                        STT(sum_, ps, y, sum_, ALU.mult, ALU.add).then_inc(mix_step, 1)
                    else:
                        if q == 0:
                            dve.wait_ge(mix_step, 8 * i + 8)
                        else:
                            dve.wait_ge(mix_last, i + 1)
                        STT(x2[p], ps, y, x2[p], ALU.mult, ALU.add).then_inc(mix_last if q == 0 else mix_done, 1)

            def mix_sums(i, p):
                dve.wait_ge(mix_step, 8 * i + 7)
                TT(x2[p], x2[p], mixed, ALU.add).then_inc(mix_step, 1)

            def lo(i, dst, src, hi, hi_done, done_):
                dve.wait_ge(hi_done, i)
                TT(dst, src, hi.bitcast(F32), ALU.subtract).then_inc(done_, 1)

            def weigh(i, p):
                dve.wait_ge(base_done, i + 1)
                if not (isinstance(i, int) and i == 0):
                    dve.wait_ge(turnr_done, i)
                y = Y1[:, bass.ds(i, 1), :].rearrange("p a e -> p (a e)").unsqueeze(2).broadcast_to([P, E, R])
                low = l2_ps[p][:, D:D + E * R]
                STT(ranks.rearrange("p (e r) -> p e r", e=E), low.rearrange("p (e r) -> p e r", e=E),
                    ALPHA / R, y, ALU.mult, ALU.mult).then_inc(ranks_done, 1)

            def ranks_lo(i):
                lo(i + 1, rl, turnr_ps, rh, rh_done, rl_done)

            def keep(i, p):
                dve.wait_ge(mix_done, i + 1)
                TT(home(i), x2[p], b2s, ALU.add).then_inc(kept_done, 1)

            def finish2(i, p):
                dve.wait_ge(lora_done, i + 1)
                dve.wait_ge(kept_done, i + 1)
                TT(home(i), l2_ps[p][:, 0:D], home(i), ALU.add).then_inc(x3_done, 1)

            def step(i, p, before=True, after=True, after2=True, first=False, second=False):
                if before:
                    keep(i - 1, 1 - p)
                if before and not second:
                    ranks_lo(i - 2)
                mix_start(i, p, first=first or second)
                mix(i, p, 0)
                if before:
                    lo(i, x2l[1 - p], turnx_ps[:, 0:D], x2h[1 - p], x2h_done, x2l_done)
                mix(i, p, 1)
                if after:
                    lo(i + 2, x1l[1 - p], turn1_ps[:, 0:D], x1h[1 - p], x1h_done, x1l_done)
                if before and not second:
                    finish2(i - 2, p)
                mix(i, p, 2)
                if before:
                    weigh(i - 1, 1 - p)
                mix_sums(i, p)
                if after2:
                    join(i + 2, p)
                mix(i, p, 3)

            dve.wait_ge(cond_wide_in, 32)
            dve.wait_ge(biases_in, 32)
            join(0, 0, first=True)
            join(1, 1, first=True)
            lo(1, x1l[0], turn1_ps[:, 0:D], x1h[0], x1h_done, x1l_done)
            step(0, 0, before=False, first=True)
            step(1, 1, second=True)
            with dve.Fori(1, NSH // 2 - 1) as pair:
                step(2 * pair, 0)
                step(2 * pair + 1, 1)
            step(NSH - 2, 0, after2=False)
            step(NSH - 1, 1, after=False, after2=False)
            keep(NSH - 1, 1)
            ranks_lo(NSH - 2)
            finish2(NSH - 2, 0)
            lo(NSH, x2l[1], turnx_ps[:, 0:D], x2h[1], x2h_done, x2l_done)
            weigh(NSH - 1, 1)
            ranks_lo(NSH - 1)
            finish2(NSH - 1, 1)

            def hidden3(i, first=False):
                dve.wait_ge(silu_done, i + 1)
                dve.wait_ge(gate3_done, i + 1)
                if not first:
                    dve.wait_ge(turnh_done, i)
                TT(hid3, gate3_ps[:, :], act3, ALU.mult).then_inc(hid3_done, 1)

            def finish3(i, p, first=False):
                batches = [dve.value_load(place[0:1, bass.ds(SLOTS0 + 2 * i + j, 1)], min_val=0, max_val=NONE)
                           for j in range(2)]
                dve.wait_ge(down3_done, i + 2)
                if not first:
                    dve.wait_ge(out_done[p], 16 * (i - p))
                for j, b in enumerate(batches):
                    half = slice(S * j, S * (j + 1))
                    op = TT(result[p][half, :], out3_ps[half, 0:D],
                            acc[half, bass.ds(b, 1), :].rearrange("p a d -> p (a d)"), ALU.add)
                op.then_inc(y_done, 1)

            def step3(i, p, before=True, after=True, first=False, early=False):
                if before:
                    lo(i, h3l, turnh_ps[:, :], h3h, h3h_done, h3l_done)
                hidden3(i, first=first)
                if after:
                    lo(i + 2, x3l, turn3_ps[:, 0:D], x3h, x3h_done, x3l_done)
                if before:
                    finish3(i - 1, 1 - p, first=early)

            dve.wait_ge(spread_done, NSH)
            lo(1, x3l, turn3_ps[:, 0:D], x3h, x3h_done, x3l_done)
            step3(0, 0, before=False, first=True)
            step3(1, 1, early=True)
            step3(2, 0, early=True)
            step3(3, 1)
            with dve.Fori(2, G3 // 2 - 1) as pair:
                step3(2 * pair, 0)
                step3(2 * pair + 1, 1)
            step3(G3 - 2, 0)
            step3(G3 - 1, 1, after=False)
            lo(G3, h3l, turnh_ps[:, :], h3h, h3h_done, h3l_done)
            finish3(G3 - 1, 1)


def kernel(x, cond_8, L0_cond_skill_gate, L0_cond_skill_up, L0_cond_skill_down, L0_cond_shared_gate,
           L0_cond_shared_up, L0_cond_shared_down, L1_cond_weight, L1_cond_mask, L1_cond_bias,
           L2_cond_W_base, L2_cond_b_base, L2_cond_As, L2_cond_Bs, L3_cond_W_up, L3_cond_b_up,
           L3_cond_W_gate, L3_cond_b_gate, L3_cond_W_down, L3_cond_b_down):
    import numpy as np

    import concourse.bacc as bacc
    from concourse.bass_utils import run_bass_kernel_spmd

    def rows(w):
        w = np.asarray(w)
        return np.swapaxes(w.reshape(*w.shape[:-2], w.shape[-2] // P, P, w.shape[-1]), -3, -2)

    x = np.asarray(x)
    gate = rows(np.concatenate([np.asarray(L0_cond_shared_gate)[None], np.asarray(L0_cond_skill_gate)]))
    up = rows(np.concatenate([np.asarray(L0_cond_shared_up)[None], np.asarray(L0_cond_skill_up)]))
    down = rows(np.concatenate([np.asarray(L0_cond_shared_down)[None], np.asarray(L0_cond_skill_down)]))
    parts = []
    for h in range(2):
        parts += [gate[..., I0 // 2 * h:I0 // 2 * (h + 1)].reshape(E + 1, P, PIECE),
                  up[..., I0 // 2 * h:I0 // 2 * (h + 1)].reshape(E + 1, P, PIECE),
                  down[:, :, 4 * h:4 * (h + 1)].reshape(E + 1, P, PIECE)]
    w1 = np.swapaxes(rows(np.swapaxes(np.asarray(L1_cond_weight), 1, 2)), 0, 1)
    w1 = np.swapaxes(w1, 1, 2).reshape(P, DC * E * D)
    mask = rows(np.asarray(L1_cond_mask).T).reshape(P, DC * D)
    w2 = np.concatenate([np.concatenate([rows(np.asarray(L2_cond_W_base).T),
                                         rows(np.asarray(L2_cond_As).reshape(E * R, D).T)],
                                        axis=2).reshape(P, DC * (D + E * R)),
                         np.swapaxes(np.asarray(L2_cond_Bs), 1, 2).reshape(E * R, D)], axis=1)
    w3 = np.concatenate([rows(np.swapaxes(np.asarray(w), 1, 2)).reshape(E, P, PIECE)
                         for w in (L3_cond_W_up, L3_cond_W_gate, L3_cond_W_down)], axis=2)
    b3 = np.concatenate([np.asarray(b) for b in (L3_cond_b_up, L3_cond_b_gate, L3_cond_b_down)], axis=1)
    ins = {
        "x": x,
        "xT": rows(np.swapaxes(x, 1, 2)),
        "cond": np.asarray(cond_8),
        "w0": np.concatenate(parts, axis=2),
        "w1": w1, "mask": mask, "b1": np.asarray(L1_cond_bias),
        "w2": w2, "b2": np.asarray(L2_cond_b_base),
        "w3": w3, "b3": b3,
    }
    ins = {k: np.ascontiguousarray(v) for k, v in ins.items()}
    nc = bacc.Bacc("TRN2", target_bir_lowering=False, num_devices=1, dynamic_dma_scratch_size=DMA_RING)
    aps = {k: nc.dram_tensor(f"in_{k}", v.shape, mybir.dt.from_np(v.dtype), kind="ExternalInput").ap()
           for k, v in ins.items()}
    out = nc.dram_tensor("out_rows", (NB + SLOTS3, S, D), F32, kind="ExternalOutput").ap()
    build(nc, **aps, out=out)
    result = run_bass_kernel_spmd(nc, [{f"in_{k}": v for k, v in ins.items()}], core_ids=[0])
    return result.results[0]["out_rows"][:NB]
```
